# Optimizing a Trainium2 kernel written in Bass

```python
import numpy as np
import jax
import jax.numpy as jnp

def _softmax(x, axis=-1):
    return jax.nn.softmax(x, axis=axis)
def _gelu(x):
    return jax.nn.gelu(x, approximate=True)
def _silu(x):
    return jax.nn.silu(x)
def _sigmoid(x):
    return jax.nn.sigmoid(x)
def _layernorm(x, axis=-1, eps=1e-5):
    m = jnp.mean(x, axis=axis, keepdims=True)
    v = jnp.var(x, axis=axis, keepdims=True)
    return (x - m) / jnp.sqrt(v + eps)
def _scatter_add(tgt, idx, src, axis=0):
    return tgt.at[idx].add(src)
def _segment_sum(src, seg, n):
    return jax.ops.segment_sum(src, seg, n)

kernel_name = 'mk_adj_preln_d4_adj_512_728a98'

def setup_inputs(seed: int = 0):
    np.random.seed(seed)
    _w = jnp.asarray
    def _rec_inputs():
        import jax
        import jax.numpy as jnp
        _gk = jax.random.key(seed)
        x = 7.22e-05 + 1 * jax.random.normal(jax.random.fold_in(_gk, 1), (128, 128, 512), jnp.float32)
        _a = jax.random.bernoulli(jax.random.fold_in(_gk, 2), 0.0625, (128, 128, 128))
        _a = jnp.logical_or(_a, jnp.swapaxes(_a, -1, -2))
        _a = jnp.logical_or(_a, jnp.eye(128, dtype=bool))
        adj = _a.astype(jnp.int32)
        return x, adj
    x, adj = _rec_inputs()
    def _L0_gnn_setup():
        import jax, jax.numpy as jnp
        import numpy as np
        ALPHA = 0.2
        NEG_INF = -1000000000.0
        key = jax.random.key(seed)
        k1, k2, k3, k4, k5 = jax.random.split(key, 5)
        B, N, F_IN, F_OUT = (16, 1024, 512, 512)
        graph_input = jax.random.normal(k1, (B, N, F_IN), dtype=jnp.float32)
        adj = jax.random.randint(k2, (B, N, N), 0, 2, dtype=jnp.int32)
        W = jax.random.normal(k3, (F_OUT, F_IN), dtype=jnp.float32) * (1.414 / np.sqrt(F_IN))
        a1 = jax.random.normal(k4, (F_OUT, 1), dtype=jnp.float32) * 0.1
        a2 = jax.random.normal(k5, (F_OUT, 1), dtype=jnp.float32) * 0.1
        return {'graph_input': graph_input, 'adj': adj, 'W': W, 'a1': a1, 'a2': a2}
    _L0_gnn_all = _L0_gnn_setup()
    _L0_gnn_in = {k: v for k, v in _L0_gnn_all.items() if k in ('W', 'a1', 'a2', )}
    del _L0_gnn_all

    def _L1_gnn_setup():
        import jax, jax.numpy as jnp
        import numpy as np
        NEG_INF = -1000000000.0
        NEG_SLOPE = 0.2

        def gat_layer(x, mask, W, a_src, a_dst, bias, concat):
            B, N, _ = x.shape
            H, F = a_src.shape
            xl = (x @ W).reshape(B, N, H, F)
            asrc = jnp.einsum('bnhf,hf->bnh', xl, a_src)
            adst = jnp.einsum('bnhf,hf->bnh', xl, a_dst)
            e = jax.nn.leaky_relu(asrc[:, :, None, :] + adst[:, None, :, :], NEG_SLOPE)
            e = jnp.where(mask[..., None], e, NEG_INF)
            attn = jax.nn.softmax(e, axis=1)
            out = jnp.einsum('bsdh,bshf->bdhf', attn, xl)
            if concat:
                out = out.reshape(B, N, H * F)
            else:
                out = out.mean(axis=2)
            return out + bias
        key = jax.random.key(seed)
        ks = jax.random.split(key, 10)
        B, N, Din, Fh, H, Dout = (8, 1024, 512, 256, 4, 512)
        s = 0.05
        return {'adj': jax.random.randint(ks[0], (B, N, N), 0, 2, dtype=jnp.int32), 'x': jax.random.normal(ks[1], (B, N, Din), dtype=jnp.float32), 'W1': jax.random.normal(ks[2], (Din, H * Fh), dtype=jnp.float32) * s, 'att_src1': jax.random.normal(ks[3], (H, Fh), dtype=jnp.float32) * s, 'att_dst1': jax.random.normal(ks[4], (H, Fh), dtype=jnp.float32) * s, 'b1': jax.random.normal(ks[5], (H * Fh,), dtype=jnp.float32) * s, 'W2': jax.random.normal(ks[6], (H * Fh, Dout), dtype=jnp.float32) * s, 'att_src2': jax.random.normal(ks[7], (1, Dout), dtype=jnp.float32) * s, 'att_dst2': jax.random.normal(ks[8], (1, Dout), dtype=jnp.float32) * s, 'b2': jax.random.normal(ks[9], (Dout,), dtype=jnp.float32) * s}
    _L1_gnn_all = _L1_gnn_setup()
    _L1_gnn_in = {k: v for k, v in _L1_gnn_all.items() if k in ('W1', 'att_src1', 'att_dst1', 'b1', 'W2', 'att_src2', 'att_dst2', 'b2', )}
    del _L1_gnn_all

    def _L2_gnn_setup():
        import jax, jax.numpy as jnp
        import numpy as np
        NEG_SLOPE = 0.2
        key = jax.random.key(seed)
        k1, k2, k3, k4, k5 = jax.random.split(key, 5)
        B, N, H = (8, 1024, 512)
        node_features = jax.random.normal(k1, (B, N, H), dtype=jnp.float32)
        adjacency_matrix = jax.random.randint(k2, (B, N, N), 0, 2, dtype=jnp.int32)
        scale = 1.0 / np.sqrt(2 * H)
        attn_w_src = jax.random.uniform(k3, (H,), jnp.float32, -scale, scale)
        attn_w_dst = jax.random.uniform(k4, (H,), jnp.float32, -scale, scale)
        attn_b = jax.random.uniform(k5, (1,), jnp.float32, -scale, scale)
        return {'node_features': node_features, 'adjacency_matrix': adjacency_matrix, 'attn_w_src': attn_w_src, 'attn_w_dst': attn_w_dst, 'attn_b': attn_b}
    _L2_gnn_all = _L2_gnn_setup()
    _L2_gnn_in = {k: v for k, v in _L2_gnn_all.items() if k in ('attn_w_src', 'attn_w_dst', 'attn_b', )}
    del _L2_gnn_all

    def _L3_gnn_setup():
        import jax, jax.numpy as jnp
        import numpy as np
        NEG_INF = -1e+30
        NEG_SLOPE = 0.2
        key = jax.random.key(seed)
        k1, k2, k3, k4, k5 = jax.random.split(key, 5)
        B, N, D, H = (2, 2048, 512, 8)
        k = D // H
        return {'x': jax.random.normal(k1, (B, N, D), dtype=jnp.float32), 'A': jax.random.randint(k2, (B, N, N), 0, 2, dtype=jnp.int32), 'W_proj': jax.random.normal(k3, (D, D), dtype=jnp.float32) * (1.0 / np.sqrt(D)), 'W_att': jax.random.normal(k4, (H, 2 * k), dtype=jnp.float32) * (1.0 / np.sqrt(2 * k)), 'b_att': jax.random.normal(k5, (H,), dtype=jnp.float32) * 0.01}
    _L3_gnn_all = _L3_gnn_setup()
    _L3_gnn_in = {k: v for k, v in _L3_gnn_all.items() if k in ('W_proj', 'W_att', 'b_att', )}
    del _L3_gnn_all

    return {
        "x": x,
        "adj": adj,
        "L0_gnn_W": _L0_gnn_in["W"],
        "L0_gnn_a1": _L0_gnn_in["a1"],
        "L0_gnn_a2": _L0_gnn_in["a2"],
        "L1_gnn_W1": _L1_gnn_in["W1"],
        "L1_gnn_att_src1": _L1_gnn_in["att_src1"],
        "L1_gnn_att_dst1": _L1_gnn_in["att_dst1"],
        "L1_gnn_b1": _L1_gnn_in["b1"],
        "L1_gnn_W2": _L1_gnn_in["W2"],
        "L1_gnn_att_src2": _L1_gnn_in["att_src2"],
        "L1_gnn_att_dst2": _L1_gnn_in["att_dst2"],
        "L1_gnn_b2": _L1_gnn_in["b2"],
        "L2_gnn_attn_w_src": _L2_gnn_in["attn_w_src"],
        "L2_gnn_attn_w_dst": _L2_gnn_in["attn_w_dst"],
        "L2_gnn_attn_b": _L2_gnn_in["attn_b"],
        "L3_gnn_W_proj": _L3_gnn_in["W_proj"],
        "L3_gnn_W_att": _L3_gnn_in["W_att"],
        "L3_gnn_b_att": _L3_gnn_in["b_att"],
    }

def reference(x, adj, L0_gnn_W, L0_gnn_a1, L0_gnn_a2, L1_gnn_W1, L1_gnn_att_src1, L1_gnn_att_dst1, L1_gnn_b1, L1_gnn_W2, L1_gnn_att_src2, L1_gnn_att_dst2, L1_gnn_b2, L2_gnn_attn_w_src, L2_gnn_attn_w_dst, L2_gnn_attn_b, L3_gnn_W_proj, L3_gnn_W_att, L3_gnn_b_att):
    import jax
    import jax.numpy as jnp
    def _L0_gnn_ref(graph_input, adj, W, a1, a2):
        import jax, jax.numpy as jnp
        import numpy as np
        ALPHA = 0.2
        NEG_INF = -1000000000.0
        h = jnp.einsum('bnf,of->bno', graph_input, W)
        f1 = h @ a1
        f2 = h @ a2
        e = f1 + jnp.swapaxes(f2, 1, 2)
        e = jax.nn.leaky_relu(e, negative_slope=ALPHA)
        scores = jnp.where(adj == 0, NEG_INF, e)
        attn = jax.nn.softmax(scores, axis=2)
        h_prime = jnp.einsum('bnm,bmf->bnf', attn, graph_input)
        return jax.nn.elu(h_prime)

    def _L1_gnn_ref(adj, x, W1, att_src1, att_dst1, b1, W2, att_src2, att_dst2, b2):
        import jax, jax.numpy as jnp
        import numpy as np
        NEG_INF = -1000000000.0
        NEG_SLOPE = 0.2

        def gat_layer(x, mask, W, a_src, a_dst, bias, concat):
            B, N, _ = x.shape
            H, F = a_src.shape
            xl = (x @ W).reshape(B, N, H, F)
            asrc = jnp.einsum('bnhf,hf->bnh', xl, a_src)
            adst = jnp.einsum('bnhf,hf->bnh', xl, a_dst)
            e = jax.nn.leaky_relu(asrc[:, :, None, :] + adst[:, None, :, :], NEG_SLOPE)
            e = jnp.where(mask[..., None], e, NEG_INF)
            attn = jax.nn.softmax(e, axis=1)
            out = jnp.einsum('bsdh,bshf->bdhf', attn, xl)
            if concat:
                out = out.reshape(B, N, H * F)
            else:
                out = out.mean(axis=2)
            return out + bias
        B, N, _ = adj.shape
        mask = (adj > 0) | jnp.eye(N, dtype=bool)[None]
        h = jax.nn.elu(gat_layer(x, mask, W1, att_src1, att_dst1, b1, concat=True))
        h = gat_layer(h, mask, W2, att_src2, att_dst2, b2, concat=False)
        return h

    def _L2_gnn_ref(node_features, adjacency_matrix, attn_w_src, attn_w_dst, attn_b):
        import jax, jax.numpy as jnp
        import numpy as np
        NEG_SLOPE = 0.2
        B, N, H = node_features.shape
        s_src = jnp.einsum('bnh,h->bn', node_features, attn_w_src)
        s_dst = jnp.einsum('bnh,h->bn', node_features, attn_w_dst)
        scores = s_src[:, :, None] + s_dst[:, None, :] + attn_b[0]
        scores = jax.nn.leaky_relu(scores, negative_slope=NEG_SLOPE)
        adj = adjacency_matrix.astype(jnp.float32) + jnp.eye(N, dtype=jnp.float32)[None]
        scores = jnp.where(adj == 0, -jnp.inf, scores)
        attn = jax.nn.softmax(scores, axis=-1)
        return jnp.einsum('bij,bjh->bih', attn, node_features)

    def _L3_gnn_ref(x, A, W_proj, W_att, b_att):
        import jax, jax.numpy as jnp
        import numpy as np
        NEG_INF = -1e+30
        NEG_SLOPE = 0.2
        B, N, _ = x.shape
        H, two_k = W_att.shape
        k = two_k // 2
        xp = jnp.einsum('bnd,do->bno', x, W_proj)
        xh = xp.reshape(B, N, H, k).transpose(0, 2, 1, 3)
        a_src = jnp.einsum('bhnk,hk->bhn', xh, W_att[:, :k])
        a_dst = jnp.einsum('bhnk,hk->bhn', xh, W_att[:, k:])
        scores = a_src[:, :, :, None] + a_dst[:, :, None, :] + b_att[None, :, None, None]
        scores = jax.nn.leaky_relu(scores, negative_slope=NEG_SLOPE)
        mask = (A > 0)[:, None, :, :]
        scores = jnp.where(mask, scores, NEG_INF)
        att = jax.nn.softmax(scores, axis=-1)
        out = jax.nn.relu(jnp.einsum('bhij,bhjk->bhik', att, xh))
        return out.transpose(0, 2, 1, 3).reshape(B, N, H * k)

    h = jnp.maximum(_layernorm(x, axis=-1), 0.0)
    x = x + _L0_gnn_ref(h, adj, L0_gnn_W, L0_gnn_a1, L0_gnn_a2)
    h = jnp.maximum(_layernorm(x, axis=-1), 0.0)
    x = x + _L1_gnn_ref(adj, h, L1_gnn_W1, L1_gnn_att_src1, L1_gnn_att_dst1, L1_gnn_b1, L1_gnn_W2, L1_gnn_att_src2, L1_gnn_att_dst2, L1_gnn_b2)
    h = jnp.maximum(_layernorm(x, axis=-1), 0.0)
    x = x + _L2_gnn_ref(h, adj, L2_gnn_attn_w_src, L2_gnn_attn_w_dst, L2_gnn_attn_b)
    h = jnp.maximum(_layernorm(x, axis=-1), 0.0)
    x = x + _L3_gnn_ref(h, adj, L3_gnn_W_proj, L3_gnn_W_att, L3_gnn_b_att)
    return x


_drawn_inputs = setup_inputs


def setup_inputs(seed=0):
    import zlib

    import numpy as np

    out = dict(_drawn_inputs(seed))
    spreads = {}
    factors = {'L1_gnn_att_dst1': 26.533,
     'L1_gnn_att_src2': 6.733,
     'L1_gnn_att_dst2': 24.449,
     'L2_gnn_attn_w_src': 8.0,
     'L2_gnn_attn_w_dst': 5.482,
     'L3_gnn_W_att': 4.6,
     'L3_gnn_b_att': 200.0}
    for name, (base, spread) in spreads.items():
        noise = np.random.default_rng([zlib.crc32(name.encode()), seed]).standard_normal(out[name].shape)
        drawn = base * np.exp(spread * noise) if base else spread * noise
        out[name] = jnp.asarray(drawn.astype(out[name].dtype))
    for name, factor in factors.items():
        out[name] = (out[name] * factor).astype(out[name].dtype)
    return out
```

```python
from contextlib import ExitStack

import concourse.bass as bass
from concourse import mybir

ALU = mybir.AluOpType
ACT = mybir.ActivationFunctionType
AX_X = mybir.AxisListType.X
F32 = mybir.dt.float32
F32R = mybir.dt.float32r
BF16 = mybir.dt.bfloat16
I32 = mybir.dt.int32

P = 128
SKEW = 6
UNROLL = 6
PEELED = SKEW + 2
SLOPE = 0.2
BIG = 5.0e9
EPS = 1e-5


class Graph:

    def __init__(self, turn, skew):
        self.turn, self.skew = turn, skew
        self.offset = turn.step - skew

    @property
    def live(self):
        return self.turn.loop is not None or 0 <= self.offset < self.turn.graphs

    def slot(self, ring):
        return self.offset % ring

    def made(self, back=0):
        return self.turn.value(UNROLL, self.offset + 1 - back)

    def turns_of(self, ring, each, back=0):
        return self.turn.value(UNROLL // ring * each, ((self.offset - back) // ring + 1) * each)

    def index(self):
        return self.turn.value(UNROLL, self.offset)


class Turn:
    def __init__(self, eng, graphs, step, loop=None, kept=None):
        self.eng, self.graphs, self.step, self.loop, self.kept = eng, graphs, step, loop, kept

    def graph(self, skew):
        return Graph(self, skew)

    def value(self, scale, add):
        if self.loop is None:
            return max(0, add)
        if (scale, add) not in self.kept:
            self.kept[scale, add] = self.eng.snap(self.loop * scale + add)
        return self.kept[scale, add]


def run_turns(eng, graphs, turn_body, before=0):
    turns = graphs + SKEW
    loops = (graphs - PEELED) // UNROLL
    for n in range(PEELED):
        turn_body(Turn(eng, graphs, n))
    if loops > 1:
        with eng.Fori(0, loops) as loop:
            kept = {}
            for j in range(UNROLL):
                turn_body(Turn(eng, graphs, PEELED + j, loop, kept))
    else:
        loops = 0
    for n in range(PEELED + loops * UNROLL, turns):
        turn_body(Turn(eng, graphs, n))


def build(nc, x, adj, a0_w, a0_a1, a0_a2, w1, att_src1, att_dst1, b1, w2, att_src2, att_dst2, b2,
          attn_src, attn_dst, attn_b, w_proj, w_att, b_att, ident_in, out):
    G, N, D = x.shape
    H1, F1 = att_src1.shape
    D1 = H1 * F1
    H3 = w_att.shape[0]
    K3 = w_att.shape[1] // 2
    assert N == P and D == 512 and D1 % P == 0 and H3 * K3 == D
    C = D // P
    C1 = D1 // P
    E1 = D1 + 2 * H1
    B1 = E1 // 3
    E2 = D + 4
    B2 = E2 // 2
    B3 = D // 2 + H3
    HB = H3 // 2
    KA = K3 + 1
    NMIN = 96
    assert E1 % 6 == 0 and B1 <= 512

    with ExitStack() as ctx:
        def sb(name, shape, dt=F32):
            return ctx.enter_context(nc.sbuf_tensor(name, shape, dt))

        def psum(name, shape):
            return ctx.enter_context(nc.psum_tensor(name, shape, F32))

        sems = {}

        def sem(name):
            if name not in sems:
                sems[name] = ctx.enter_context(nc.semaphore(name))
            return sems[name]

        ident = sb("ident", [P, P])
        nident = sb("nident", [P, P])
        identb = sb("identb", [P, P], BF16)
        offdiag = sb("offdiag", [P, P], BF16)
        nhalf = sb("nhalf", [P, 1])
        w1_hi = sb("w1_hi", [P, C, E1], F32R)
        w1_lo = sb("w1_lo", [P, C, E1], F32R)
        w2_hi = sb("w2_hi", [P, C1, E2], F32R)
        w2_lo = sb("w2_lo", [P, C1, E2], F32R)
        w3_hi = sb("w3_hi", [P, C, 2 * B3], F32R)
        w3_lo = sb("w3_lo", [P, C, 2 * B3], F32R)
        b1_row = sb("b1_row", [P, E1])
        b2_row = sb("b2_row", [P, E2])
        s_row = {0: sb("s_row0", [P, D]), 2: sb("s_row2", [P, D])}
        t_row = {0: sb("t_row0", [P, D]), 2: sb("t_row2", [P, D])}
        attn_b_all = sb("attn_b_all", [P, 1])
        b_att_all = sb("b_att_all", [P, H3])

        XR, MR, X1R, X3R, OR = 3, 6, 3, 2, 2
        x_in = sb("x_in", [P, XR, D])
        adj_in = sb("adj_in", [P, XR, P], I32)
        mask = sb("mask", [P, MR, P], BF16)
        mask_loop = sb("mask_loop", [P, MR, P], BF16)
        x1 = sb("x1", [P, X1R, D])
        x2 = sb("x2", [P, D])
        x3 = sb("x3", [P, X3R, D])
        out_sb = sb("out_sb", [P, OR, D])

        h = [sb(f"h{i}", [P, D]) for i in range(4)]
        bn = [sb(f"bn{i}", [P, 6]) for i in range(4)]
        mv = [sb(f"mv{i}", [P, 2]) for i in range(4)]
        rs = [sb(f"rs{i}", [P, 3]) for i in range(4)]
        st = {i: sb(f"st{i}", [P, 2]) for i in (0, 2)}
        product = sb("product", [P, 2, D])
        one = ("L0", "L1b", "L2")
        nl1 = {k: sb(f"nl_{k}", [P, 2, P]) for k in one}
        nm1 = {k: sb(f"nm_{k}", [P, 1]) for k in one}
        p1 = {k: sb(f"p_{k}", [P, P]) for k in one}
        pT1 = {k: sb(f"pT_{k}", [P, P]) for k in one}
        sum1 = {k: sb(f"sum_{k}", [P, 2]) for k in one}
        hT_hi = {k: sb(f"hT_hi{k}", [P, D], F32R) for k in (1, 3)}
        hT_lo = {k: sb(f"hT_lo{k}", [P, D], F32R) for k in (1, 3)}
        xl = sb("xl", [P, E1])
        nlB = sb("nlB", [P, 2, H1, P])
        nmB = sb("nmB", [P, H1])
        dB = sb("dB", [P, H1, P])
        pB = sb("pB", [P, H1, P])
        sumB = sb("sumB", [P, 2, H1])
        pTB = sb("pTB", [P, H1, P])
        elu = sb("elu", [P, C1, P])
        g1 = sb("g1", [P, C1, P])
        g_hi = sb("g_hi", [P, C1, P], F32R)
        g_lo = sb("g_lo", [P, C1, P], F32R)
        xl2 = sb("xl2", [P, E2])
        xa = sb("xa", [P, H3 * KA + NMIN - KA])
        st3 = sb("st3", [P, 2, H3])
        nlE = sb("nlE", [P, H3, P])
        nmE = sb("nmE", [P, H3])
        pE = sb("pE", [P, H3, P])
        pTE = sb("pTE", [P, H3, P])
        rcE = sb("rcE", [P, 2, HB])
        rE = sb("rE", [P, D])

        bank_a = psum("bank_a", [P, 512])
        bank_b = psum("bank_b", [P, 3, 512])
        bank_c = psum("bank_c", [P, 2, 512])
        bank_e = psum("bank_e", [P, 2, 512])

        xa_heads = xa[:, 0:H3 * KA].rearrange("p (h k) -> p h k", h=H3)

        stage = [nlB[:].rearrange("p a h n -> p (a h n)"), elu[:].rearrange("p c n -> p (c n)")]
        att1 = [pE[:].rearrange("p h n -> p (h n)"), pTE[:].rearrange("p h n -> p (h n)")]
        att2 = [x_in[:, 0, :], x_in[:, 1, :]]
        att3 = [x1[:, 0, :], x1[:, 1, :]]
        multiplied = nlE[:].rearrange("p h n -> p (h n)")
        ext = sb("ext", [P, 2, 16])
        w_chunks = [("w1", c) for c in range(C)] + [("w2", c) for c in range(C1)] + [("w3", c) for c in range(C)]
        a0_stage = x3

        block = ctx.enter_context(nc.Block())

        def w_parts(kind):
            if kind == "w1":
                return w1_hi, w1_lo, [(0, 0, D1)], (D1, D1 + H1), H1, att1
            if kind == "w2":
                return w2_hi, w2_lo, [(0, 0, D)], (D, D + 1), 1, att2
            return w3_hi, w3_lo, [(0, 0, D // 2), (B3, D // 2, D // 2)], (D // 2, D // 2 + B3), H3, att3

        w_dram = {"w1": w1.rearrange("(c p) n -> c p n", p=P), "w2": w2.rearrange("(c p) n -> c p n", p=P),
                  "w3": w_proj.rearrange("(c p) n -> c p n", p=P)}
        w_cols = {"w1": D1, "w2": D, "w3": D}

        @block.sync
        def _(sp):
            consts_in, w_in = sem("consts_in"), [sem("w_in0"), sem("w_in1")]

            def row(src):
                return src.rearrange("(a n) -> a n", a=1)

            sp.dma_start(ident[:], ident_in).then_inc(consts_in, 16)
            for dst, src in (
                (att1[1][:, 0:D1], row(att_src1.rearrange("h f -> (h f)"))),
                (att1[0][:, 0:D1], row(att_dst1.rearrange("h f -> (h f)"))),
                (att2[1], att_src2), (att2[0], att_dst2),
                (b1_row[:, 0:D1], row(b1)), (b2_row[:, 0:D], row(b2)),
                (s_row[2][:], row(attn_src)), (t_row[2][:], row(attn_dst)),
                (attn_b_all[:], row(attn_b)), (b_att_all[:], row(b_att)),
            ):
                sp.dma_start(dst, src.to_broadcast([P, src.shape[1]])).then_inc(consts_in, 16)
            for i in range(2):
                src = w_att[:, i * K3:(i + 1) * K3].rearrange("(a h) k -> a h k", a=1)
                sp.dma_start(att3[i].rearrange("p (h k) -> p h k", h=H3),
                             src.to_broadcast([P, H3, K3])).then_inc(consts_in, 16)
            sp.dma_start(st3[:, 0, 0:C], a0_a1.rearrange("(p c) a -> p (c a)", p=P)).then_inc(consts_in, 16)
            sp.dma_start(st3[:, 1, 0:C], a0_a2.rearrange("(p c) a -> p (c a)", p=P)).then_inc(consts_in, 16)
            for c in range(C):
                dst = (x3[:, c, :] if c < 2 else out_sb[:, c - 2, :])
                sp.dma_start(dst, a0_w.rearrange("(p c) f -> c p f", p=P)[c]).then_inc(consts_in, 16)
            for n, (kind, c) in enumerate(w_chunks):
                if n >= 2:
                    sp.wait_ge(sem("w_split"), n - 1)
                sp.dma_start(stage[n % 2][:, 0:w_cols[kind]], w_dram[kind][c]).then_inc(w_in[n % 2], 16)
            sp.wait_ge(sem("w_split"), len(w_chunks))

            def load(g):
                s = g.slot(XR)
                sp.wait_ge(sem("x1_made"), g.made(XR))
                sp.wait_ge(sem("mask_made"), g.made(XR))
                sp.dma_start(x_in[:, s, :], x[g.index()]).then_inc(sem(f"x_loaded{s}"), 16)
                sp.dma_start(adj_in[:, s, :], adj[g.index()]).then_inc(sem(f"x_loaded{s}"), 16)

            def store(g):
                s = g.slot(OR)
                sp.wait_ge(sem("out_made"), g.made())
                sp.dma_start(out[g.index()], out_sb[:, s, :]).then_inc(sem(f"out_stored{s}"), 16)

            def turn(t):
                if t.graph(0).live:
                    load(t.graph(0))
                if t.graph(6).live:
                    store(t.graph(6))

            run_turns(sp, G, turn)
            for s in range(OR):
                sp.wait_ge(sem(f"out_stored{s}"), 16 * len(range(s, G, OR)))

        @block.tensor
        def _(pe):
            mm = nc.tensor.matmul

            pe.wait_ge(sem("consts_in"), 16 * CONSTS)
            for i in range(2):
                for c in range(C):
                    w = x3[:, c, :] if c < 2 else out_sb[:, c - 2, :]
                    last = mm(bank_e[:, i, :], st3[:, i, c:c + 1].to_broadcast([P, P]), w,
                              start=(c == 0), stop=(c == C - 1))
            last.then_inc(sem("u0_made"), 1)
            pe.wait_ge(sem("setup_done"), 3)

            def masks_and_t(bank, mask_l, mask_r, t_cols):
                heads = len(t_cols)
                mm(bank[:, 0:heads * P], mask_l, mask_r, start=True, stop=False)
                for k, t_col in enumerate(t_cols):
                    last = mm(bank[:, k * P:(k + 1) * P], t_col.to_broadcast([P, P]), nident[:],
                              start=False, stop=(k == heads - 1))
                return last

            def direct(m, heads):
                if heads == 1:
                    return identb[:], m
                return identb[:], m.rearrange("p (a n) -> p a n", a=1).to_broadcast([P, heads, P])

            def turned(m, heads):
                if heads == 1:
                    return m, identb[:]
                return m, identb[:].rearrange("p (a n) -> p a n", a=1).to_broadcast([P, heads, P])

            def to_columns(bank, src):
                for c in range(C):
                    last = nc.tensor.transpose(bank[:, c * P:(c + 1) * P], src[:, c * P:(c + 1) * P], ident[:])
                return last

            def project(banks, width, chunks, total, hi, lo, w_hi, w_lo):
                for c in chunks:
                    for n, (a, w) in enumerate(((hi, w_hi), (hi, w_lo), (lo, w_hi))):
                        for b in range(len(banks)):
                            last = mm(banks[b][:, 0:width], a(c), w[:, c, b * width:(b + 1) * width],
                                      start=(c == 0 and n == 0), stop=(c == total - 1 and n == 2))
                return last

            def turn(t):
                A, B, Cg, Dg, E, Z = [t.graph(k) for k in (1, 2, 3, 4, 5, 6)]

                if Z.live:
                    for i in range(2):
                        pe.wait_ge(sem(f"L3_exp{i}"), Z.made())
                        for k in range(HB):
                            head = i * HB + k
                            last = nc.tensor.transpose(bank_e[:, i, k * P:(k + 1) * P], pE[:, head, :], ident[:])
                        last.then_inc(sem(f"L3_turned{i}"), 1)
                if A.live:
                    pe.wait_ge(sem("st_made0"), A.made())
                    pe.wait_ge(sem("masks_made"), A.made())
                    if t.loop is None:
                        pe.wait_ge(sem("x1_made"), A.made(1))
                    pe.wait_ge(sem("x3_made"), A.made(4))
                    m_l, m_r = direct(mask[:, A.slot(MR), :], 1)
                    masks_and_t([bank_a][0], m_l, m_r, [st[0][:, 1:2]]).then_inc(sem("L0_scores"), 1)
                if Z.live:
                    for i in range(2):
                        pe.wait_ge(sem(f"L3_pT{i}"), Z.made())
                        for k in range(HB):
                            head = i * HB + k
                            last = mm(bank_e[:, i, k * KA:k * KA + NMIN], pTE[:, head, :],
                                      xa[:, head * KA:head * KA + NMIN], start=True, stop=True)
                    last.then_inc(sem("L3_out"), 1)
                if B.live:
                    pe.wait_ge(sem("h_made1"), B.made())
                    pe.wait_ge(sem("L1a_pT"), B.made(1))
                    to_columns(bank_b[:, 2, :], h[1][:]).then_inc(sem("L1a_hT"), 1)
                if A.live:
                    pe.wait_ge(sem("L0_exp"), A.made())
                    nc.tensor.transpose(bank_a[:, 0:P], p1["L0"][:], ident[:]).then_inc(sem("L0_turned"), 1)
                if Cg.live:
                    if t.loop is None and t.step == 3:
                        pe.wait_ge(sem("w_split"), C + C1)
                    pe.wait_ge(sem("g_lo_first"), Cg.made())
                    pe.wait_ge(sem("x2_made"), Cg.made(1))
                    project([bank_c[:, 0, :], bank_c[:, 1, :]], B2, range(C1 // 2), C1,
                            lambda c: g_hi[:, c, :], lambda c: g_lo[:, c, :], w2_hi, w2_lo)
                if B.live:
                    if t.loop is None and t.step == 2:
                        pe.wait_ge(sem("w_split"), C)
                    pe.wait_ge(sem("L1a_hT_lo"), B.made())
                    pe.wait_ge(sem("g_made_last"), B.made(1))
                    project([bank_b[:, b, :] for b in range(3)], B1, range(C), C,
                            lambda c: hT_hi[1][:, c * P:(c + 1) * P], lambda c: hT_lo[1][:, c * P:(c + 1) * P],
                            w1_hi, w1_lo).then_inc(sem("L1a_xl"), 1)
                if A.live:
                    pe.wait_ge(sem("L0_pT"), A.made())
                    mm(bank_a[:], pT1["L0"][:], h[0][:], start=True, stop=True).then_inc(sem("L0_out"), 1)
                if E.live:
                    pe.wait_ge(sem("h_made3"), E.made())
                    pe.wait_ge(sem("out_read"), E.made(1))
                    to_columns(bank_e[:, 0, :], h[3][:]).then_inc(sem("L3_hT"), 1)
                if B.live:
                    pe.wait_ge(sem("xl_made"), B.made())
                    m_l, m_r = turned(mask_loop[:, B.slot(MR), :], H1)
                    masks_and_t(bank_b[:, 2, :], m_l, m_r,
                                [xl[:, D1 + H1 + k:D1 + H1 + k + 1] for k in range(H1)]).then_inc(sem("L1a_scores"), 1)
                if Dg.live:
                    pe.wait_ge(sem("st_made2"), Dg.made())
                    if A.live:
                        pe.wait_ge(sem("x1_made"), A.made())
                    else:
                        pe.wait_ge(sem("x3_made"), Dg.made(1))
                    m_l, m_r = direct(mask_loop[:, Dg.slot(MR), :], 1)
                    masks_and_t(bank_a, m_l, m_r, [st[2][:, 1:2]]).then_inc(sem("L2_scores"), 1)
                if Cg.live:
                    pe.wait_ge(sem("g_lo_last"), Cg.made())
                    project([bank_c[:, 0, :], bank_c[:, 1, :]], B2, range(C1 // 2, C1), C1,
                            lambda c: g_hi[:, c, :], lambda c: g_lo[:, c, :], w2_hi, w2_lo).then_inc(sem("L1b_xl"), 1)
                if E.live:
                    if t.loop is None and t.step == 5:
                        pe.wait_ge(sem("w_split"), len(w_chunks))
                    pe.wait_ge(sem("L3_hT_lo"), E.made())
                    project([bank_e[:, 0, :], bank_e[:, 1, :]], B3, range(C), C,
                            lambda c: hT_hi[3][:, c * P:(c + 1) * P], lambda c: hT_lo[3][:, c * P:(c + 1) * P],
                            w3_hi, w3_lo).then_inc(sem("L3_xl"), 1)
                if Dg.live:
                    pe.wait_ge(sem("L2_exp"), Dg.made())
                    nc.tensor.transpose(bank_a[:, 0:P], p1["L2"][:], ident[:]).then_inc(sem("L2_turned"), 1)
                if Cg.live:
                    pe.wait_ge(sem("xl2_made"), Cg.made())
                    m_l, m_r = turned(mask_loop[:, Cg.slot(MR), :], 1)
                    masks_and_t(bank_c[:, 0, :], m_l, m_r, [xl2[:, D + 1:D + 2]]).then_inc(sem("L1b_scores"), 1)
                if Dg.live:
                    pe.wait_ge(sem("L2_pT"), Dg.made())
                    mm(bank_a[:], pT1["L2"][:], h[2][:], start=True, stop=True).then_inc(sem("L2_out"), 1)

                def scores3(i):
                    if E.live:
                        pe.wait_ge(sem("xa_made"), E.made())
                        m_l, m_r = direct(mask[:, E.slot(MR), :], HB)
                        masks_and_t(bank_e[:, i, :], m_l, m_r,
                                    [st3[:, 1, i * HB + k:i * HB + k + 1] for k in range(HB)])\
                            .then_inc(sem(f"L3_scores{i}"), 1)

                scores3(0)
                if B.live:
                    pe.wait_ge(sem("L1a_prob"), B.made())
                    for k in range(H1):
                        last = nc.tensor.transpose(bank_b[:, 2, k * P:(k + 1) * P], pB[:, k, :], ident[:])
                    last.then_inc(sem("L1a_turned"), 1)
                scores3(1)
                if Cg.live:
                    pe.wait_ge(sem("L1b_exp"), Cg.made())
                    nc.tensor.transpose(bank_c[:, 0, 0:P], p1["L1b"][:], ident[:]).then_inc(sem("L1b_turned"), 1)
                if B.live:
                    pe.wait_ge(sem("L1a_pT"), B.made())
                    for c in range(C1):
                        bank, at = c // (C1 // 2), c % (C1 // 2)
                        last = mm(bank_b[:, bank, at * P:(at + 1) * P], xl[:, c * P:(c + 1) * P],
                                  pTB[:, c * P // F1, :], start=(at == 0), stop=(at == C1 // 2 - 1))
                        if at == C1 // 2 - 1:
                            last.then_inc(sem(f"L1a_out{bank}"), 1)
                if Cg.live:
                    pe.wait_ge(sem("L1b_pT"), Cg.made())
                    mm(bank_c[:, 1, :], pT1["L1b"][:], xl2[:, 0:D], start=True, stop=True)\
                        .then_inc(sem("L1b_out"), 1)

            run_turns(pe, G, turn)

        @block.scalar
        def _(act):
            activation = nc.scalar.activation

            for n, (kind, c) in enumerate(w_chunks):
                hi, lo, cols, (s_at, t_at), heads, att = w_parts(kind)
                act.wait_ge(sem("w_in0" if n % 2 == 0 else "w_in1"), 16 * (n // 2 + 1))
                for to, frm, count in cols:
                    activation(hi[:, c, to:to + count], stage[n % 2][:, frm:frm + count], ACT.Copy)\
                        .then_inc(sem("w_hi"), 1)
                act.wait_ge(sem("ext_made"), n + 1)
                activation(hi[:, c, s_at:s_at + heads], ext[:, n % 2, 0:heads], ACT.Copy).then_inc(sem("w_hi"), 1)
                activation(hi[:, c, t_at:t_at + heads], ext[:, n % 2, 8:8 + heads], ACT.Copy).then_inc(sem("w_hi"), 1)
                if kind == "w2":
                    activation(hi[:, c, D + 2:E2], ext[:, n % 2, 8:10], ACT.Copy, scale=0.0).then_inc(sem("w_hi"), 1)

            def norm(layer, g, free):
                src = {0: x_in[:, g.slot(XR), :], 1: x1[:, g.slot(X1R), :], 2: x2[:], 3: x3[:, g.slot(X3R), :]}[layer]
                act.wait_ge(sem(f"rs_made{layer}"), g.made())
                act.wait_ge(sem(free[0]), g.made(free[1]))
                activation(h[layer][:], src, ACT.Relu, bias=rs[layer][:, 2:3], scale=rs[layer][:, 1:2])\
                    .then_inc(sem(f"h_made{layer}"), 1)

            def exp_one(key, g):
                act.wait_ge(sem(f"{key}_min"), g.made())
                act.wait_ge(sem(f"{key}_turned"), g.made(1))
                act.wait_ge(sem(f"{key}_recip"), g.made(1))
                activation(p1[key][:], nl1[key][:, 1, :], ACT.Exp, bias=nm1[key][:], scale=-1.0,
                           accum_out=sum1[key][:, 0:1]).then_inc(sem(f"{key}_exp"), 1)

            def pT_one(key, g, bank):
                act.wait_ge(sem(f"{key}_turned"), g.made())
                act.wait_ge(sem(f"{key}_out"), g.made(1))
                activation(pT1[key][:], bank, ACT.Copy).then_inc(sem(f"{key}_pT"), 1)

            def turn(t):
                N0, A, B, Cg, Dg, E, Z = [t.graph(k) for k in range(7)]
                if Z.live:
                    for i in range(2):
                        act.wait_ge(sem(f"L3_turned{i}"), Z.made())
                        act.wait_ge(sem("L3_out"), Z.made(1))
                        activation(pTE[:, i * HB:(i + 1) * HB, :],
                                   bank_e[:, i, :].rearrange("p (k n) -> p k n", k=HB), ACT.Copy)\
                            .then_inc(sem(f"L3_pT{i}"), 1)
                if Dg.live:
                    norm(2, Dg, ("L2_out", 1))
                if A.live:
                    exp_one("L0", A)
                if B.live:
                    act.wait_ge(sem("L1a_hT"), B.made())
                    act.wait_ge(sem("L1a_xl"), B.made(1))
                    activation(hT_hi[1][:], bank_b[:, 2, :], ACT.Copy).then_inc(sem("L1a_hT_hi"), 1)
                if A.live:
                    pT_one("L0", A, bank_a[:, 0:P])
                if E.live:
                    act.wait_ge(sem("L3_hT"), E.made())
                    act.wait_ge(sem("L3_xl"), E.made(1))
                    activation(hT_hi[3][:], bank_e[:, 0, :], ACT.Copy).then_inc(sem("L3_hT_hi"), 1)
                if N0.live:
                    norm(0, N0, ("L0_out", 1))
                if A.live:
                    norm(1, A, ("L1a_hT", 1))
                if Dg.live:
                    exp_one("L2", Dg)
                    pT_one("L2", Dg, bank_a[:, 0:P])
                if B.live:
                    act.wait_ge(sem("L1a_shifted"), B.made())
                    act.wait_ge(sem("L1a_prob"), B.made(1))
                    activation(dB[:], dB[:], ACT.Exp, scale=-1.0).then_inc(sem("L1a_exp"), 1)
                if E.live:
                    act.wait_ge(sem("st3_made"), E.made())
                    act.wait_ge(sem("L3_out"), E.made(1))
                    src = bank_e[:, :, 0:D // 2].rearrange("p b (k n) -> p b k n", k=HB)
                    activation(xa_heads[:, :, 0:K3].rearrange("p (b k) n -> p b k n", b=2), src, ACT.Copy)\
                        .then_inc(sem("xa_made"), 1)
                if Cg.live:
                    exp_one("L1b", Cg)
                if B.live:
                    act.wait_ge(sem("L1a_turned"), B.made())
                    act.wait_ge(sem("L1a_out1"), B.made(1))
                    activation(pTB[:], bank_b[:, 2, :].rearrange("p (k n) -> p k n", k=H1), ACT.Copy)\
                        .then_inc(sem("L1a_pT"), 1)
                if Cg.live:
                    pT_one("L1b", Cg, bank_c[:, 0, 0:P])
                if Dg.live:
                    norm(3, Dg, ("L3_hT", 1))

                def elu_exp(i):
                    if B.live:
                        act.wait_ge(sem(f"L1a_out{i}"), B.made())
                        act.wait_ge(sem(("g_made_first", "g_made_last")[i]), B.made(1))
                        half = slice(i * (C1 // 2), (i + 1) * (C1 // 2))
                        activation(elu[:, half, :], bank_b[:, i, :].rearrange("p (c n) -> p c n", c=C1 // 2),
                                   ACT.Exp).then_inc(sem(f"elu_exp{i}"), 1)

                def g_high(i):
                    if B.live:
                        act.wait_ge(sem(("g_made_first", "g_made_last")[i]), B.made())
                        act.wait_ge(sem("L1b_xl"), B.made(1))
                        half = slice(i * (C1 // 2), (i + 1) * (C1 // 2))
                        activation(g_hi[:, half, :], g1[:, half, :], ACT.Copy).then_inc(sem(f"g_hi{i}"), 1)

                def exp3(i):
                    if E.live:
                        act.wait_ge(sem(f"L3_shifted{i}"), E.made())
                        act.wait_ge(sem(f"L3_turned{i}"), E.made(1))
                        activation(pE[:, i * HB:(i + 1) * HB, :], nlE[:, i * HB:(i + 1) * HB, :], ACT.Exp,
                                   scale=-1.0).then_inc(sem(f"L3_exp{i}"), 1)

                elu_exp(0)
                elu_exp(1)
                g_high(0)
                exp3(0)
                g_high(1)
                exp3(1)

            run_turns(act, G, turn)

        @block.vector
        def _(dve):
            tt, ts, stt = nc.vector.tensor_tensor, nc.vector.tensor_scalar, nc.vector.scalar_tensor_tensor

            dve.wait_ge(sem("consts_in"), 16 * CONSTS)
            ts(nident[:], ident[:], -1.0, None, ALU.mult).then_inc(sem("setup_done"), 1)
            nc.vector.tensor_copy(identb[:], ident[:]).then_inc(sem("setup_done"), 1)
            ts(offdiag[:], ident[:], -1.0, 1.0, ALU.mult, ALU.add).then_inc(sem("setup_vec"), 1)
            nc.vector.memset(nhalf[:], -0.5).then_inc(sem("setup_vec"), 1)
            ts(att1[0][:, 0:D1], att1[0][:, 0:D1], -1.0, None, ALU.mult).then_inc(sem("setup_vec"), 1)
            ts(att2[0], att2[0], -1.0, None, ALU.mult).then_inc(sem("setup_vec"), 1)
            ts(att3[0], att3[0], -1.0, None, ALU.mult).then_inc(sem("setup_vec"), 1)
            ts(s_row[2][:], s_row[2][:], -1.0, None, ALU.mult).then_inc(sem("setup_vec"), 1)
            nc.vector.memset(b1_row[:, D1:E1], 0.0).then_inc(sem("setup_vec"), 1)
            nc.vector.memset(b2_row[:, D:E2], 0.0).then_inc(sem("setup_vec"), 1)
            nc.vector.memset(xa[:], 1.0).then_inc(sem("setup_done"), 1)
            dve.wait_ge(sem("u0_made"), 1)
            ts(s_row[0][:], bank_e[:, 0, :], -1.0, None, ALU.mult).then_inc(sem("setup_vec"), 1)
            nc.vector.tensor_copy(t_row[0][:], bank_e[:, 1, :]).then_inc(sem("setup_vec"), 1)
            dve.wait_ge(sem("setup_vec"), 10)

            his = 0
            for n, (kind, c) in enumerate(w_chunks):
                hi, lo, cols, (s_at, t_at), heads, att = w_parts(kind)
                width = w_cols[kind]
                dve.wait_ge(sem("w_in0" if n % 2 == 0 else "w_in1"), 16 * (n // 2 + 1))
                dve.wait_ge(sem("w_split"), n)
                for i in range(2):
                    if i or n:
                        dve.wait_ge(sem("ext_sums"), 2 * n + i)
                    tt(multiplied[:, 0:width], stage[n % 2][:, 0:width], att[i][:, 0:width], ALU.mult)\
                        .then_inc(sem("ext_products"), 1)
                    dve.wait_ge(sem("ext_products"), 2 * n + i + 1)
                    last = nc.vector.tensor_reduce(
                        ext[:, n % 2, 8 * i:8 * i + heads],
                        multiplied[:, 0:width].rearrange("p (h k) -> p h k", h=heads), AX_X, ALU.add)
                    last.then_inc(sem("ext_sums"), 1)
                dve.wait_ge(sem("ext_sums"), 2 * n + 2)
                nc.vector.tensor_copy(ext[:, n % 2, 8 + heads:10], ext[:, n % 2, 0:2 - heads])\
                    .then_inc(sem("ext_made"), 1) if heads < 2 else \
                    nc.vector.memset(nm1["L0"][:], 0.0).then_inc(sem("ext_made"), 1)
                his += len(cols) + 2 + (kind == "w2")
                dve.wait_ge(sem("w_hi"), his)
                dve.wait_ge(sem("ext_made"), n + 1)
                parts = [(to, stage[n % 2][:, frm:frm + count], count) for to, frm, count in cols]
                parts += [(s_at, ext[:, n % 2, 0:heads], heads), (t_at, ext[:, n % 2, 8:8 + heads], heads)]
                if kind == "w2":
                    parts.append((D + 2, hi[:, c, D + 2:E2].bitcast(F32), 2))
                for k, (to, whole, count) in enumerate(parts):
                    last = tt(lo[:, c, to:to + count], whole, hi[:, c, to:to + count].bitcast(F32), ALU.subtract)
                last.then_inc(sem("w_split"), 1)
            dve.wait_ge(sem("w_split"), len(w_chunks))

            def stats(layer, g, src):
                nc.vector.bn_stats(bn[layer][:], src).then_inc(sem(f"bn_made{layer}"), 1)
                dve.wait_ge(sem(f"bn_made{layer}"), g.made())
                dve.wait_ge(sem(f"rs_made{layer}"), g.made(1))
                dve.sem_inc(sem("passed_dve"), 1)
                nc.vector.bn_aggr(mv[layer][:], bn[layer][:]).then_inc(sem(f"mv_made{layer}"), 1)

            def score_columns(layer, g, scores):
                dve.wait_ge(sem(f"h_made{layer}"), g.made())
                dve.wait_ge(sem(scores), g.made(1))
                for i, (row, sign) in enumerate(((s_row, 1.0), (t_row, 1.0))):
                    last = nc.vector.tensor_tensor_reduce(product[:, i, :], h[layer][:], row[layer][:], sign, 0.0,
                                                          ALU.mult, ALU.add, st[layer][:, i:i + 1])
                last.then_inc(sem(f"st_made{layer}"), 1)

            def softmax_one(key, g, bank, ns, bias=None):
                dve.wait_ge(sem(f"{key}_scores"), g.made())
                dve.wait_ge(sem(f"{key}_exp"), g.made(1))
                if bias is None:
                    ts(nl1[key][:, 0, :], bank, ns, None, ALU.add).then_inc(sem(f"{key}_v"), 1)
                else:
                    ts(nl1[key][:, 0, :], bank, ns, bias, ALU.add, ALU.subtract).then_inc(sem(f"{key}_v"), 1)
                dve.wait_ge(sem(f"{key}_v"), g.made())
                stt(nl1[key][:, 1, :], nl1[key][:, 0, :], SLOPE, nl1[key][:, 0, :], ALU.mult, ALU.min)\
                    .then_inc(sem(f"{key}_nl"), 1)
                dve.wait_ge(sem(f"{key}_nl"), g.made())
                nc.vector.tensor_reduce(nm1[key][:], nl1[key][:, 1, :], AX_X, ALU.min).then_inc(sem(f"{key}_min"), 1)

            def recip_one(key, g):
                dve.wait_ge(sem(f"{key}_exp"), g.made())
                nc.vector.reciprocal(sum1[key][:, 1:2], sum1[key][:, 0:1]).then_inc(sem(f"{key}_recip"), 1)

            def residual(key, g, bank, src, dst, made):
                dve.wait_ge(sem(f"{key}_out"), g.made())
                dve.wait_ge(sem(f"{key}_recip"), g.made())
                stt(dst, bank, sum1[key][:, 1:2], src, ALU.mult, ALU.add).then_inc(sem(made), 1)

            def turn(t):
                N0, A, B, Cg, Dg, E, Z = [t.graph(k) for k in range(7)]
                if Dg.live:
                    dve.wait_ge(sem("x2_made"), Dg.made())
                    stats(2, Dg, x2[:])
                if A.live:
                    softmax_one("L0", A, bank_a[:, 0:P], st[0][:, 0:1])
                if Z.live:
                    dve.wait_ge(sem("L3_out"), Z.made())
                    wide = bank_e[:, :, 0:HB * KA].rearrange("p b (k n) -> p b k n", k=HB)
                    nc.vector.reciprocal(rcE[:], wide[:, :, :, K3]).then_inc(sem("L3_recip"), 1)
                    dve.wait_ge(sem("L3_recip"), Z.made())
                    dve.wait_ge(sem("out_made"), Z.made(1))
                    r4 = rE[:].rearrange("p (b k n) -> p b k n", b=2, k=HB)
                    rc4 = rcE[:].rearrange("p b (k a) -> p b k a", a=1).to_broadcast([P, 2, HB, K3])
                    tt(r4, wide[:, :, :, 0:K3], rc4, ALU.mult).then_inc(sem("out_read"), 1)
                    dve.wait_ge(sem("out_read"), Z.made())
                    dve.wait_ge(sem(f"out_stored{Z.slot(OR)}"), Z.turns_of(OR, 16, OR))
                    stt(out_sb[:, Z.slot(OR), :], rE[:], 0.0, x3[:, Z.slot(X3R), :], ALU.max, ALU.add)\
                        .then_inc(sem("out_made"), 1)
                if Dg.live:
                    score_columns(2, Dg, "L2_scores")
                if B.live:
                    dve.wait_ge(sem("L1a_hT_hi"), B.made())
                    dve.wait_ge(sem("L1a_xl"), B.made(1))
                    tt(hT_lo[1][:], bank_b[:, 2, :], hT_hi[1][:].bitcast(F32), ALU.subtract)\
                        .then_inc(sem("L1a_hT_lo"), 1)
                if A.live:
                    recip_one("L0", A)
                if N0.live:
                    dve.wait_ge(sem(f"x_loaded{N0.slot(XR)}"), N0.turns_of(XR, 32))
                    stats(0, N0, x_in[:, N0.slot(XR), :])
                    score_columns(0, N0, "L0_scores")
                if B.live:
                    dve.wait_ge(sem("L1a_xl"), B.made())
                    dve.wait_ge(sem("L1a_out1"), B.made(1))
                    tt(xl[:].rearrange("p (b n) -> p b n", b=3), bank_b[:, :, 0:B1],
                       b1_row[:].rearrange("p (b n) -> p b n", b=3), ALU.add).then_inc(sem("xl_made"), 1)
                if A.live:
                    dve.wait_ge(sem("h_made1"), A.made(3))
                    residual("L0", A, bank_a[:], x_in[:, A.slot(XR), :], x1[:, A.slot(X1R), :], "x1_made")
                    dve.wait_ge(sem("x1_made"), A.made())
                    stats(1, A, x1[:, A.slot(X1R), :])
                if E.live:
                    dve.wait_ge(sem("L3_hT_hi"), E.made())
                    dve.wait_ge(sem("L3_xl"), E.made(1))
                    tt(hT_lo[3][:], bank_e[:, 0, :], hT_hi[3][:].bitcast(F32), ALU.subtract)\
                        .then_inc(sem("L3_hT_lo"), 1)
                if B.live:
                    dve.wait_ge(sem("L1a_scores"), B.made())
                    dve.wait_ge(sem("L1a_shifted"), B.made(1))
                    ns = xl[:, D1:D1 + H1].rearrange("p (h a) -> p h a", a=1).to_broadcast([P, H1, P])
                    tt(nlB[:, 0], bank_b[:, 2, :].rearrange("p (h n) -> p h n", h=H1), ns, ALU.add)\
                        .then_inc(sem("L1a_v"), 1)
                    dve.wait_ge(sem("L1a_v"), B.made())
                    stt(nlB[:, 1], nlB[:, 0], SLOPE, nlB[:, 0], ALU.mult, ALU.min).then_inc(sem("L1a_nl"), 1)
                    dve.wait_ge(sem("L1a_nl"), B.made())
                    nc.vector.tensor_reduce(nmB[:], nlB[:, 1], AX_X, ALU.min).then_inc(sem("L1a_min"), 1)
                if Dg.live:
                    softmax_one("L2", Dg, bank_a[:, 0:P], st[2][:, 0:1], attn_b_all[:])
                if B.live:
                    dve.wait_ge(sem("L1a_exp"), B.made())
                    dve.wait_ge(sem("L1a_prob"), B.made(1))
                    nc.vector.tensor_reduce(sumB[:, 0, :], dB[:], AX_X, ALU.add).then_inc(sem("L1a_sum"), 1)
                    dve.wait_ge(sem("L1a_sum"), B.made())
                    nc.vector.reciprocal(sumB[:, 1, :], sumB[:, 0, :]).then_inc(sem("L1a_recip"), 1)
                if Dg.live:
                    recip_one("L2", Dg)
                if Cg.live:
                    dve.wait_ge(sem("L1b_xl"), Cg.made())
                    dve.wait_ge(sem("L1b_out"), Cg.made(1))
                    tt(xl2[:].rearrange("p (b n) -> p b n", b=2), bank_c[:, :, 0:B2],
                       b2_row[:].rearrange("p (b n) -> p b n", b=2), ALU.add).then_inc(sem("xl2_made"), 1)
                if E.live:
                    dve.wait_ge(sem("L3_xl"), E.made())
                    dve.wait_ge(sem("L3_scores1"), E.made(1))
                    tt(st3[:, 0, :], bank_e[:, 0, D // 2:B3], b_att_all[:], ALU.subtract).then_inc(sem("st3_s"), 1)
                    nc.vector.tensor_copy(st3[:, 1, :], bank_e[:, 1, D // 2:B3]).then_inc(sem("st3_made"), 1)
                if Dg.live:
                    dve.wait_ge(sem("out_made"), Dg.made(2))
                    residual("L2", Dg, bank_a[:], x2[:], x3[:, Dg.slot(X3R), :], "x3_made")
                    dve.wait_ge(sem("x3_made"), Dg.made())
                    stats(3, Dg, x3[:, Dg.slot(X3R), :])
                if Cg.live:
                    softmax_one("L1b", Cg, bank_c[:, 0, 0:P], xl2[:, D:D + 1])
                if E.live:
                    for i in range(2):
                        dve.wait_ge(sem(f"L3_scores{i}"), E.made())
                        dve.wait_ge(sem("L3_exp1"), E.made(1))
                        dve.wait_ge(sem("st3_s"), E.made())
                        half = slice(i * HB, (i + 1) * HB)
                        ns = st3[:, 0, half].rearrange("p (h a) -> p h a", a=1).to_broadcast([P, HB, P])
                        tt(nlE[:, half, :], bank_e[:, i, :].rearrange("p (h n) -> p h n", h=HB), ns, ALU.add)\
                            .then_inc(sem(f"L3_v{i}"), 1)
                if Cg.live:
                    recip_one("L1b", Cg)
                if E.live:
                    dve.wait_ge(sem("L3_v1"), E.made())
                    stt(nlE[:], nlE[:], SLOPE, nlE[:], ALU.mult, ALU.min).then_inc(sem("L3_nl"), 1)
                    dve.wait_ge(sem("L3_nl"), E.made())
                    nc.vector.tensor_reduce(nmE[:], nlE[:], AX_X, ALU.min).then_inc(sem("L3_min"), 1)
                if B.live:
                    for i, name in enumerate(("g_made_first", "g_made_last")):
                        half = slice(i * (C1 // 2), (i + 1) * (C1 // 2))
                        dve.wait_ge(sem(f"elu_exp{i}"), B.made())
                        ts(elu[:, half, :], elu[:, half, :], 1.0, -1.0, ALU.min, ALU.add)\
                            .then_inc(sem(f"elu_clamped{i}"), 1)
                        dve.wait_ge(sem(f"elu_clamped{i}"), B.made())
                        dve.wait_ge(sem("g_lo_last"), B.made(1))
                        tt(g1[:, half, :], bank_b[:, i, :].rearrange("p (c n) -> p c n", c=C1 // 2),
                           elu[:, half, :], ALU.max).then_inc(sem(name), 1)
                    dve.wait_ge(sem("g_hi0"), B.made())
                    half = slice(0, C1 // 2)
                    tt(g_lo[:, half, :], g1[:, half, :], g_hi[:, half, :].bitcast(F32), ALU.subtract)\
                        .then_inc(sem("g_lo_first"), 1)
                if Cg.live:
                    dve.wait_ge(sem("h_made2"), Cg.made(1))
                    residual("L1b", Cg, bank_c[:, 1, :], x1[:, Cg.slot(X1R), :], x2[:], "x2_made")

            run_turns(dve, G, turn)

        @block.gpsimd
        def _(pool):
            tt, ts = nc.gpsimd.tensor_tensor, nc.gpsimd.tensor_scalar
            pool.wait_ge(sem("setup_vec"), 10)
            pool.wait_ge(sem("w_split"), len(w_chunks))

            def scale_and_bias(layer, g):
                pool.wait_ge(sem(f"mv_made{layer}"), g.made())
                pool.wait_ge(sem(f"h_made{layer}"), g.made(1))
                pool.sem_inc(sem("passed_pool"), 1)
                v, r, b = [rs[layer][:, k:k + 1] for k in range(3)]
                ts(v, mv[layer][:, 1:2], EPS, None, ALU.add).then_inc(sem(f"var_made{layer}"), 1)
                pool.wait_ge(sem(f"var_made{layer}"), g.made())
                tt(r, v, nhalf[:], ALU.pow).then_inc(sem(f"rstd_made{layer}"), 1)
                pool.wait_ge(sem(f"rstd_made{layer}"), g.made())
                pool.sem_inc(sem("passed_pool"), 1)
                ts(b, mv[layer][:, 0:1], r, -1.0, ALU.mult, ALU.mult).then_inc(sem(f"rs_made{layer}"), 1)

            def turn(t):
                N0, A, B, Cg, Dg, E, Z = [t.graph(k) for k in range(7)]
                if Dg.live:
                    scale_and_bias(2, Dg)
                if N0.live:
                    scale_and_bias(0, N0)
                    s, m = N0.slot(XR), N0.slot(MR)
                    pool.wait_ge(sem(f"x_loaded{s}"), N0.turns_of(XR, 32))
                    pool.wait_ge(sem("L3_scores1"), N0.made(MR))
                    pool.sem_inc(sem("passed_pool"), 1)
                    ts(mask[:, m, :], adj_in[:, s, :], -BIG, BIG, ALU.mult, ALU.add).then_inc(sem("mask_made"), 1)
                    pool.wait_ge(sem("mask_made"), N0.made())
                    tt(mask_loop[:, m, :], mask[:, m, :], offdiag[:], ALU.mult).then_inc(sem("masks_made"), 1)
                if A.live:
                    scale_and_bias(1, A)
                if B.live:
                    pool.wait_ge(sem("L1a_min"), B.made())
                    pool.wait_ge(sem("L1a_prob"), B.made(1))
                    nm = nmB[:].rearrange("p (h a) -> p h a", a=1).to_broadcast([P, H1, P])
                    tt(dB[:], nlB[:, 1], nm, ALU.subtract).then_inc(sem("L1a_shifted"), 1)
                    pool.wait_ge(sem("L1a_recip"), B.made())
                    pool.wait_ge(sem("L1a_turned"), B.made(1))
                    rc = sumB[:, 1, :].rearrange("p (h a) -> p h a", a=1).to_broadcast([P, H1, P])
                    tt(pB[:], dB[:], rc, ALU.mult).then_inc(sem("L1a_prob"), 1)
                if Dg.live:
                    scale_and_bias(3, Dg)
                if E.live:
                    for i in range(2):
                        half = slice(i * HB, (i + 1) * HB)
                        pool.wait_ge(sem("L3_min"), E.made())
                        nm = nmE[:, half].rearrange("p (h a) -> p h a", a=1).to_broadcast([P, HB, P])
                        tt(nlE[:, half, :], nlE[:, half, :], nm, ALU.subtract).then_inc(sem(f"L3_shifted{i}"), 1)
                if B.live:
                    pool.wait_ge(sem("g_hi1"), B.made())
                    pool.wait_ge(sem("L1b_xl"), B.made(1))
                    half = slice(C1 // 2, C1)
                    tt(g_lo[:, half, :], g1[:, half, :], g_hi[:, half, :].bitcast(F32), ALU.subtract)\
                        .then_inc(sem("g_lo_last"), 1)

            run_turns(pool, G, turn)


CONSTS = 19

_INS = ["x", "adj", "L0_gnn_W", "L0_gnn_a1", "L0_gnn_a2", "L1_gnn_W1", "L1_gnn_att_src1", "L1_gnn_att_dst1",
        "L1_gnn_b1", "L1_gnn_W2", "L1_gnn_att_src2", "L1_gnn_att_dst2", "L1_gnn_b2", "L2_gnn_attn_w_src",
        "L2_gnn_attn_w_dst", "L2_gnn_attn_b", "L3_gnn_W_proj", "L3_gnn_W_att", "L3_gnn_b_att"]


def kernel(**inputs):
    import concourse.bacc as bacc
    import numpy as np
    from concourse.bass_utils import run_bass_kernel_spmd

    nc = bacc.Bacc("TRN2", target_bir_lowering=False, num_devices=1)
    ins = {f"in_{name}": np.ascontiguousarray(inputs[name]) for name in _INS}
    ins["in_ident"] = np.eye(P, dtype=np.float32)
    aps = [nc.dram_tensor(n, a.shape, mybir.dt.from_np(a.dtype), kind="ExternalInput").ap() for n, a in ins.items()]
    out = nc.dram_tensor("out", inputs["x"].shape, F32, kind="ExternalOutput").ap()
    build(nc, *aps, out)
    r = run_bass_kernel_spmd(nc, [ins], core_ids=[0])
    return r.results[0]["out"]
```

```python
from contextlib import ExitStack

import concourse.bass as bass
from concourse import mybir

ALU = mybir.AluOpType
ACT = mybir.ActivationFunctionType
AX_X = mybir.AxisListType.X
F32 = mybir.dt.float32
F32R = mybir.dt.float32r
BF16 = mybir.dt.bfloat16
I32 = mybir.dt.int32

P = 128
SKEW = 6
UNROLL = 6
PEELED = SKEW + 2
SLOPE = 0.2
BIG = 5.0e9
EPS = 1e-5


class Graph:

    def __init__(self, turn, skew):
        self.turn, self.skew = turn, skew
        self.offset = turn.step - skew

    @property
    def live(self):
        return self.turn.loop is not None or 0 <= self.offset < self.turn.graphs

    def slot(self, ring):
        return self.offset % ring

    def made(self, back=0):
        return self.turn.value(UNROLL, self.offset + 1 - back)

    def turns_of(self, ring, each, back=0):
        return self.turn.value(UNROLL // ring * each, ((self.offset - back) // ring + 1) * each)

    def index(self):
        return self.turn.value(UNROLL, self.offset)


class Turn:
    def __init__(self, eng, graphs, step, loop=None, kept=None):
        self.eng, self.graphs, self.step, self.loop, self.kept = eng, graphs, step, loop, kept

    def graph(self, skew):
        return Graph(self, skew)

    def value(self, scale, add):
        if self.loop is None:
            return max(0, add)
        if (scale, add) not in self.kept:
            self.kept[scale, add] = self.eng.snap(self.loop * scale + add)
        return self.kept[scale, add]


def run_turns(eng, graphs, turn_body, before=0):
    turns = graphs + SKEW
    loops = (graphs - PEELED) // UNROLL
    for n in range(PEELED):
        turn_body(Turn(eng, graphs, n))
    if loops > 1:
        with eng.Fori(0, loops) as loop:
            kept = {}
            for j in range(UNROLL):
                turn_body(Turn(eng, graphs, PEELED + j, loop, kept))
    else:
        loops = 0
    for n in range(PEELED + loops * UNROLL, turns):
        turn_body(Turn(eng, graphs, n))


def build(nc, x, adj, a0_w, a0_a1, a0_a2, w1, att_src1, att_dst1, b1, w2, att_src2, att_dst2, b2,
          attn_src, attn_dst, attn_b, w_proj, w_att, b_att, ident_in, out):
    G, N, D = x.shape
    H1, F1 = att_src1.shape
    D1 = H1 * F1
    H3 = w_att.shape[0]
    K3 = w_att.shape[1] // 2
    assert N == P and D == 512 and D1 % P == 0 and H3 * K3 == D
    C = D // P
    C1 = D1 // P
    E1 = D1 + 2 * H1
    B1 = E1 // 3
    E2 = D + 4
    B2 = E2 // 2
    B3 = D // 2 + H3
    HB = H3 // 2
    KA = K3 + 1
    NMIN = 96
    assert E1 % 6 == 0 and B1 <= 512

    with ExitStack() as ctx:
        def sb(name, shape, dt=F32):
            return ctx.enter_context(nc.sbuf_tensor(name, shape, dt))

        def psum(name, shape):
            return ctx.enter_context(nc.psum_tensor(name, shape, F32))

        sems = {}

        def sem(name):
            if name not in sems:
                sems[name] = ctx.enter_context(nc.semaphore(name))
            return sems[name]

        ident = sb("ident", [P, P])
        nident = sb("nident", [P, P])
        identb = sb("identb", [P, P], BF16)
        offdiag = sb("offdiag", [P, P], BF16)
        nhalf = sb("nhalf", [P, 1])
        w1_hi = sb("w1_hi", [P, C, E1], F32R)
        w1_lo = sb("w1_lo", [P, C, E1], F32R)
        w2_hi = sb("w2_hi", [P, C1, E2], F32R)
        w2_lo = sb("w2_lo", [P, C1, E2], F32R)
        w3_hi = sb("w3_hi", [P, C, 2 * B3], F32R)
        w3_lo = sb("w3_lo", [P, C, 2 * B3], F32R)
        b1_row = sb("b1_row", [P, E1])
        b2_row = sb("b2_row", [P, E2])
        s_row = {0: sb("s_row0", [P, D]), 2: sb("s_row2", [P, D])}
        t_row = {0: sb("t_row0", [P, D]), 2: sb("t_row2", [P, D])}
        attn_b_all = sb("attn_b_all", [P, 1])
        b_att_all = sb("b_att_all", [P, H3])

        XR, MR, X1R, X3R, OR = 3, 6, 3, 2, 2
        x_in = sb("x_in", [P, XR, D])
        adj_in = sb("adj_in", [P, XR, P], I32)
        mask = sb("mask", [P, MR, P], BF16)
        mask_loop = sb("mask_loop", [P, MR, P], BF16)
        x1 = sb("x1", [P, X1R, D])
        x2 = sb("x2", [P, D])
        x3 = sb("x3", [P, X3R, D])
        out_sb = sb("out_sb", [P, OR, D])

        h = [sb(f"h{i}", [P, 2 if i == 0 else 1, D]) for i in range(4)]
        bn = [sb(f"bn{i}", [P, 6]) for i in range(4)]
        mv = [sb(f"mv{i}", [P, 2]) for i in range(4)]
        rs = [sb(f"rs{i}", [P, 3]) for i in range(4)]
        st = {i: sb(f"st{i}", [P, 2]) for i in (0, 2)}
        product = sb("product", [P, 4, D], BF16)
        one = ("L0", "L1b", "L2")
        nl1 = {k: sb(f"nl_{k}", [P, 2, P]) for k in one}
        nm1 = {k: sb(f"nm_{k}", [P, 1]) for k in one}
        p1 = {k: sb(f"p_{k}", [P, P]) for k in one}
        pT1 = {k: sb(f"pT_{k}", [P, P]) for k in one}
        sum1 = {k: sb(f"sum_{k}", [P, 2]) for k in one}
        hT_hi = {k: sb(f"hT_hi{k}", [P, D], F32R) for k in (1, 3)}
        hT_lo = {k: sb(f"hT_lo{k}", [P, D], F32R) for k in (1, 3)}
        xl = sb("xl", [P, E1])
        nlB = sb("nlB", [P, 2, H1, P])
        nmB = sb("nmB", [P, H1])
        dB = sb("dB", [P, H1, P])
        pB = sb("pB", [P, H1, P])
        sumB = sb("sumB", [P, 2, H1])
        pTB = sb("pTB", [P, H1, P])
        elu = sb("elu", [P, C1, P])
        g1 = sb("g1", [P, C1, P])
        g_hi = sb("g_hi", [P, C1, P], F32R)
        g_lo = sb("g_lo", [P, C1, P], F32R)
        xl2 = sb("xl2", [P, E2])
        xa = sb("xa", [P, H3 * KA + NMIN - KA])
        st3 = sb("st3", [P, 2, H3])
        nlE = sb("nlE", [P, H3, P])
        nmE = sb("nmE", [P, H3])
        pE = sb("pE", [P, H3, P])
        pTE = sb("pTE", [P, H3, P])
        rcE = sb("rcE", [P, 2, HB])
        rE = sb("rE", [P, D])

        bank_a = psum("bank_a", [P, 512])
        bank_b = psum("bank_b", [P, 3, 512])
        bank_c = psum("bank_c", [P, 2, 512])
        bank_e = psum("bank_e", [P, 2, 512])

        g_hi_all = g_hi[:].rearrange("p c n -> p (c n)")
        g_lo_all = g_lo[:].rearrange("p c n -> p (c n)")
        xa_heads = xa[:, 0:H3 * KA].rearrange("p (h k) -> p h k", h=H3)

        stage = [nlB[:].rearrange("p a h n -> p (a h n)"), elu[:].rearrange("p c n -> p (c n)")]
        att1 = [pE[:].rearrange("p h n -> p (h n)"), pTE[:].rearrange("p h n -> p (h n)")]
        att2 = [x_in[:, 0, :], x_in[:, 1, :]]
        att3 = [x1[:, 0, :], x1[:, 1, :]]
        multiplied = nlE[:].rearrange("p h n -> p (h n)")
        ext = sb("ext", [P, 2, 16])
        w_chunks = [("w1", c) for c in range(C)] + [("w2", c) for c in range(C1)] + [("w3", c) for c in range(C)]
        a0_stage = x3

        block = ctx.enter_context(nc.Block())

        def w_parts(kind):
            if kind == "w1":
                return w1_hi, w1_lo, [(0, 0, D1)], (D1, D1 + H1), H1, att1
            if kind == "w2":
                return w2_hi, w2_lo, [(0, 0, D)], (D, D + 1), 1, att2
            return w3_hi, w3_lo, [(0, 0, D // 2), (B3, D // 2, D // 2)], (D // 2, D // 2 + B3), H3, att3

        w_dram = {"w1": w1.rearrange("(c p) n -> c p n", p=P), "w2": w2.rearrange("(c p) n -> c p n", p=P),
                  "w3": w_proj.rearrange("(c p) n -> c p n", p=P)}
        w_cols = {"w1": D1, "w2": D, "w3": D}

        @block.sync
        def _(sp):
            consts_in, w_in = sem("consts_in"), [sem("w_in0"), sem("w_in1")]

            def row(src):
                return src.rearrange("(a n) -> a n", a=1)

            sp.dma_start(ident[:], ident_in).then_inc(consts_in, 16)
            for dst, src in (
                (att1[1][:, 0:D1], row(att_src1.rearrange("h f -> (h f)"))),
                (att1[0][:, 0:D1], row(att_dst1.rearrange("h f -> (h f)"))),
                (att2[1], att_src2), (att2[0], att_dst2),
                (b1_row[:, 0:D1], row(b1)), (b2_row[:, 0:D], row(b2)),
                (s_row[2][:], row(attn_src)), (t_row[2][:], row(attn_dst)),
                (attn_b_all[:], row(attn_b)), (b_att_all[:], row(b_att)),
            ):
                sp.dma_start(dst, src.to_broadcast([P, src.shape[1]])).then_inc(consts_in, 16)
            for i in range(2):
                src = w_att[:, i * K3:(i + 1) * K3].rearrange("(a h) k -> a h k", a=1)
                sp.dma_start(att3[i].rearrange("p (h k) -> p h k", h=H3),
                             src.to_broadcast([P, H3, K3])).then_inc(consts_in, 16)
            sp.dma_start(st3[:, 0, 0:C], a0_a1.rearrange("(p c) a -> p (c a)", p=P)).then_inc(consts_in, 16)
            sp.dma_start(st3[:, 1, 0:C], a0_a2.rearrange("(p c) a -> p (c a)", p=P)).then_inc(consts_in, 16)
            for c in range(C):
                dst = (x3[:, c, :] if c < 2 else out_sb[:, c - 2, :])
                sp.dma_start(dst, a0_w.rearrange("(p c) f -> c p f", p=P)[c]).then_inc(consts_in, 16)
            for n, (kind, c) in enumerate(w_chunks):
                if n >= 2:
                    sp.wait_ge(sem("w_split"), n - 1)
                sp.dma_start(stage[n % 2][:, 0:w_cols[kind]], w_dram[kind][c]).then_inc(w_in[n % 2], 16)
            sp.wait_ge(sem("w_split"), len(w_chunks))

            def load(g):
                s = g.slot(XR)
                sp.wait_ge(sem("x1_made"), g.made(XR))
                sp.wait_ge(sem("mask_made"), g.made(XR))
                sp.dma_start(x_in[:, s, :], x[g.index()]).then_inc(sem(f"x_loaded{s}"), 16)
                sp.dma_start(adj_in[:, s, :], adj[g.index()]).then_inc(sem(f"x_loaded{s}"), 16)

            def store(g):
                s = g.slot(OR)
                sp.wait_ge(sem("out_made"), g.made())
                sp.dma_start(out[g.index()], out_sb[:, s, :]).then_inc(sem(f"out_stored{s}"), 16)

            def turn(t):
                if t.graph(0).live:
                    load(t.graph(0))
                if t.graph(6).live:
                    store(t.graph(6))

            run_turns(sp, G, turn)
            for s in range(OR):
                sp.wait_ge(sem(f"out_stored{s}"), 16 * len(range(s, G, OR)))

        @block.tensor
        def _(pe):
            mm = nc.tensor.matmul

            pe.wait_ge(sem("consts_in"), 16 * CONSTS)
            for i in range(2):
                for c in range(C):
                    w = x3[:, c, :] if c < 2 else out_sb[:, c - 2, :]
                    last = mm(bank_e[:, i, :], st3[:, i, c:c + 1].to_broadcast([P, P]), w,
                              start=(c == 0), stop=(c == C - 1))
            last.then_inc(sem("u0_made"), 1)
            pe.wait_ge(sem("setup_done"), 3)

            def masks_and_t(bank, mask_l, mask_r, t_cols):
                heads = len(t_cols)
                mm(bank[:, 0:heads * P], mask_l, mask_r, start=True, stop=False)
                for k, t_col in enumerate(t_cols):
                    last = mm(bank[:, k * P:(k + 1) * P], t_col.to_broadcast([P, P]), nident[:],
                              start=False, stop=(k == heads - 1))
                return last

            def direct(m, heads):
                if heads == 1:
                    return identb[:], m
                return identb[:], m.rearrange("p (a n) -> p a n", a=1).to_broadcast([P, heads, P])

            def turned(m, heads):
                if heads == 1:
                    return m, identb[:]
                return m, identb[:].rearrange("p (a n) -> p a n", a=1).to_broadcast([P, heads, P])

            def to_columns(bank, src):
                for c in range(C):
                    last = nc.tensor.transpose(bank[:, c * P:(c + 1) * P], src[:, c * P:(c + 1) * P], ident[:])
                return last

            def project(banks, width, chunks, products, first, final):
                for c in chunks:
                    for n, (a, w) in enumerate(products):
                        for b, bank in banks.items():
                            last = mm(bank[:, 0:width], a[:, c * P:(c + 1) * P], w[:, c, b * width:(b + 1) * width],
                                      start=(first and c == chunks[0] and n == 0),
                                      stop=(final and c == chunks[-1] and n == len(products) - 1))
                return last

            def turn(t):
                A, B, Cg, Dg, E, Z = [t.graph(k) for k in (1, 2, 3, 4, 5, 6)]

                def turn_exp_L3():
                    if Z.live:
                        for i in range(2):
                            pe.wait_ge(sem(f"L3_exp{i}"), Z.made())
                            for k in range(HB):
                                head = i * HB + k
                                last = nc.tensor.transpose(bank_e[:, i, k * P:(k + 1) * P], pE[:, head, :], ident[:])
                            last.then_inc(sem(f"L3_turned{i}"), 1)

                def scores_L0():
                    if A.live:
                        pe.wait_ge(sem("st_made0"), A.made())
                        pe.wait_ge(sem("masks_made"), A.made())
                        if t.loop is None:
                            pe.wait_ge(sem("x1_made"), A.made(1))
                        pe.wait_ge(sem("x3_made"), A.made(4))
                        m_l, m_r = direct(mask[:, A.slot(MR), :], 1)
                        masks_and_t([bank_a][0], m_l, m_r, [st[0][:, 1:2]]).then_inc(sem("L0_scores"), 1)

                def product_L3():
                    if Z.live:
                        for i in range(2):
                            pe.wait_ge(sem(f"L3_pT{i}"), Z.made())
                            for k in range(HB):
                                head = i * HB + k
                                last = mm(bank_e[:, i, k * KA:k * KA + NMIN], pTE[:, head, :],
                                          xa[:, head * KA:head * KA + NMIN], start=True, stop=True)
                        last.then_inc(sem("L3_out"), 1)

                def turn_h1():
                    if B.live:
                        pe.wait_ge(sem("h_made1"), B.made())
                        pe.wait_ge(sem("L1a_pT"), B.made(1))
                        to_columns(bank_b[:, 2, :], h[1][:, 0, :]).then_inc(sem("L1a_hT"), 1)

                def turn_exp_L0():
                    if A.live:
                        pe.wait_ge(sem("L0_exp"), A.made())
                        nc.tensor.transpose(bank_a[:, 0:P], p1["L0"][:], ident[:]).then_inc(sem("L0_turned"), 1)

                def project_L1b_first():
                    if Cg.live:
                        if t.loop is None and t.step == 3:
                            pe.wait_ge(sem("w_split"), C + C1)
                        pe.wait_ge(sem("g_hi0"), Cg.made())
                        pe.wait_ge(sem("x2_made"), Cg.made(1))
                        banks, chunks = {0: bank_c[:, 0, :], 1: bank_c[:, 1, :]}, range(C1 // 2)
                        project(banks, B2, chunks, ((g_hi_all, w2_hi), (g_hi_all, w2_lo)), True, False)
                        pe.wait_ge(sem("g_lo_first"), Cg.made())
                        project(banks, B2, chunks, ((g_lo_all, w2_hi),), False, False)

                def project_L1a():
                    if B.live:
                        if t.loop is None and t.step == 2:
                            pe.wait_ge(sem("w_split"), C)
                        pe.wait_ge(sem("L1a_hT_hi"), B.made())
                        pe.wait_ge(sem("g_made_last"), B.made(1))
                        two, last = {0: bank_b[:, 0, :], 1: bank_b[:, 1, :]}, {2: bank_b[:, 2, :]}
                        high = ((hT_hi[1], w1_hi), (hT_hi[1], w1_lo))
                        low = ((hT_lo[1], w1_hi),)
                        project(two, B1, range(C), high, True, False)
                        pe.wait_ge(sem("L1a_hT_lo"), B.made())
                        project(two, B1, range(C), low, False, True)
                        project(last, B1, range(C), high + low, True, True).then_inc(sem("L1a_xl"), 1)

                def product_L0():
                    if A.live:
                        pe.wait_ge(sem("L0_pT"), A.made())
                        mm(bank_a[:], pT1["L0"][:], h[0][:, A.slot(2), :], start=True, stop=True).then_inc(sem("L0_out"), 1)

                def turn_h3():
                    if E.live:
                        pe.wait_ge(sem("h_made3"), E.made())
                        pe.wait_ge(sem("out_read"), E.made(1))
                        to_columns(bank_e[:, 0, :], h[3][:, 0, :]).then_inc(sem("L3_hT"), 1)

                def scores_L1a():
                    if B.live:
                        pe.wait_ge(sem("xl_made"), B.made())
                        m_l, m_r = turned(mask_loop[:, B.slot(MR), :], H1)
                        masks_and_t(bank_b[:, 2, :], m_l, m_r,
                                    [xl[:, D1 + H1 + k:D1 + H1 + k + 1] for k in range(H1)]).then_inc(sem("L1a_scores"), 1)

                def scores_L2():
                    if Dg.live:
                        pe.wait_ge(sem("st_made2"), Dg.made())
                        if A.live:
                            pe.wait_ge(sem("x1_made"), A.made())
                        else:
                            pe.wait_ge(sem("x3_made"), Dg.made(1))
                        m_l, m_r = direct(mask_loop[:, Dg.slot(MR), :], 1)
                        masks_and_t(bank_a, m_l, m_r, [st[2][:, 1:2]]).then_inc(sem("L2_scores"), 1)

                def project_L1b_last():
                    if Cg.live:
                        pe.wait_ge(sem("g_hi1"), Cg.made())
                        pe.wait_ge(sem("g_lo_last"), Cg.made())
                        project({0: bank_c[:, 0, :], 1: bank_c[:, 1, :]}, B2, range(C1 // 2, C1),
                                ((g_hi_all, w2_hi), (g_hi_all, w2_lo), (g_lo_all, w2_hi)), False, True)\
                            .then_inc(sem("L1b_xl"), 1)

                def project_L3():
                    if E.live:
                        if t.loop is None and t.step == 5:
                            pe.wait_ge(sem("w_split"), len(w_chunks))
                        pe.wait_ge(sem("L3_hT_hi"), E.made())
                        high = ((hT_hi[3], w3_hi), (hT_hi[3], w3_lo))
                        low = ((hT_lo[3], w3_hi),)
                        project({1: bank_e[:, 1, :]}, B3, range(C), high, True, False)
                        pe.wait_ge(sem("L3_hT_lo"), E.made())
                        project({1: bank_e[:, 1, :]}, B3, range(C), low, False, True)
                        project({0: bank_e[:, 0, :]}, B3, range(C), high + low, True, True).then_inc(sem("L3_xl"), 1)

                def turn_exp_L2():
                    if Dg.live:
                        pe.wait_ge(sem("L2_exp"), Dg.made())
                        nc.tensor.transpose(bank_a[:, 0:P], p1["L2"][:], ident[:]).then_inc(sem("L2_turned"), 1)

                def scores_L1b():
                    if Cg.live:
                        pe.wait_ge(sem("xl2_made"), Cg.made())
                        m_l, m_r = turned(mask_loop[:, Cg.slot(MR), :], 1)
                        masks_and_t(bank_c[:, 0, :], m_l, m_r, [xl2[:, D + 1:D + 2]]).then_inc(sem("L1b_scores"), 1)

                def product_L2():
                    if Dg.live:
                        pe.wait_ge(sem("L2_pT"), Dg.made())
                        mm(bank_a[:], pT1["L2"][:], h[2][:, 0, :], start=True, stop=True).then_inc(sem("L2_out"), 1)

                def scores3(i):
                    if E.live:
                        pe.wait_ge(sem("xa_made"), E.made())
                        m_l, m_r = direct(mask[:, E.slot(MR), :], HB)
                        masks_and_t(bank_e[:, i, :], m_l, m_r,
                                    [st3[:, 1, i * HB + k:i * HB + k + 1] for k in range(HB)])\
                            .then_inc(sem(f"L3_scores{i}"), 1)

                def turn_prob_L1a():
                    if B.live:
                        pe.wait_ge(sem("L1a_prob"), B.made())
                        for k in range(H1):
                            last = nc.tensor.transpose(bank_b[:, 2, k * P:(k + 1) * P], pB[:, k, :], ident[:])
                        last.then_inc(sem("L1a_turned"), 1)

                def turn_exp_L1b():
                    if Cg.live:
                        pe.wait_ge(sem("L1b_exp"), Cg.made())
                        nc.tensor.transpose(bank_c[:, 0, 0:P], p1["L1b"][:], ident[:]).then_inc(sem("L1b_turned"), 1)

                def product_L1a():
                    if B.live:
                        pe.wait_ge(sem("L1a_pT"), B.made())
                        for c in range(C1):
                            bank, at = c // (C1 // 2), c % (C1 // 2)
                            last = mm(bank_b[:, bank, at * P:(at + 1) * P], xl[:, c * P:(c + 1) * P],
                                      pTB[:, c * P // F1, :], start=(at == 0), stop=(at == C1 // 2 - 1))
                            if at == C1 // 2 - 1:
                                last.then_inc(sem(f"L1a_out{bank}"), 1)

                def product_L1b():
                    if Cg.live:
                        pe.wait_ge(sem("L1b_pT"), Cg.made())
                        mm(bank_c[:, 1, :], pT1["L1b"][:], xl2[:, 0:D], start=True, stop=True)\
                            .then_inc(sem("L1b_out"), 1)

                scores_L0()
                turn_h1()
                project_L1b_first()
                project_L1a()
                turn_exp_L0()
                turn_exp_L3()
                product_L0()
                product_L3()
                scores_L1a()
                turn_h3()
                project_L1b_last()
                scores_L2()
                project_L3()
                scores_L1b()
                turn_exp_L2()
                scores3(0)
                turn_prob_L1a()
                product_L2()
                turn_exp_L1b()
                product_L1a()
                product_L1b()
                scores3(1)

            run_turns(pe, G, turn)

        @block.scalar
        def _(act):
            activation = nc.scalar.activation

            for n, (kind, c) in enumerate(w_chunks):
                hi, lo, cols, (s_at, t_at), heads, att = w_parts(kind)
                act.wait_ge(sem("w_in0" if n % 2 == 0 else "w_in1"), 16 * (n // 2 + 1))
                for to, frm, count in cols:
                    activation(hi[:, c, to:to + count], stage[n % 2][:, frm:frm + count], ACT.Copy)\
                        .then_inc(sem("w_hi"), 1)
                act.wait_ge(sem("ext_made"), n + 1)
                activation(hi[:, c, s_at:s_at + heads], ext[:, n % 2, 0:heads], ACT.Copy).then_inc(sem("w_hi"), 1)
                activation(hi[:, c, t_at:t_at + heads], ext[:, n % 2, 8:8 + heads], ACT.Copy).then_inc(sem("w_hi"), 1)
                if kind == "w2":
                    activation(hi[:, c, D + 2:E2], ext[:, n % 2, 8:10], ACT.Copy, scale=0.0).then_inc(sem("w_hi"), 1)

            def norm(layer, g, free):
                src = {0: x_in[:, g.slot(XR), :], 1: x1[:, g.slot(X1R), :], 2: x2[:], 3: x3[:, g.slot(X3R), :]}[layer]
                act.wait_ge(sem(f"rs_made{layer}"), g.made())
                act.wait_ge(sem(free[0]), g.made(free[1]))
                activation(h[layer][:, g.slot(2) if layer == 0 else 0, :], src, ACT.Relu, bias=rs[layer][:, 2:3], scale=rs[layer][:, 1:2])\
                    .then_inc(sem(f"h_made{layer}"), 1)

            def exp_one(key, g):
                act.wait_ge(sem(f"{key}_min"), g.made())
                act.wait_ge(sem(f"{key}_turned"), g.made(1))
                act.wait_ge(sem(f"{key}_recip"), g.made(1))
                activation(p1[key][:], nl1[key][:, 1, :], ACT.Exp, bias=nm1[key][:], scale=-1.0,
                           accum_out=sum1[key][:, 0:1]).then_inc(sem(f"{key}_exp"), 1)

            def pT_one(key, g, bank):
                act.wait_ge(sem(f"{key}_turned"), g.made())
                act.wait_ge(sem(f"{key}_out"), g.made(1))
                activation(pT1[key][:], bank, ACT.Copy).then_inc(sem(f"{key}_pT"), 1)

            def turn(t):
                N0, A, B, Cg, Dg, E, Z = [t.graph(k) for k in range(7)]

                def pT_L3():
                    if Z.live:
                        for i in range(2):
                            act.wait_ge(sem(f"L3_turned{i}"), Z.made())
                            act.wait_ge(sem("L3_out"), Z.made(1))
                            activation(pTE[:, i * HB:(i + 1) * HB, :],
                                       bank_e[:, i, :].rearrange("p (k n) -> p k n", k=HB), ACT.Copy)\
                                .then_inc(sem(f"L3_pT{i}"), 1)

                def norm2():
                    if Dg.live:
                        norm(2, Dg, ("L2_out", 1))

                def exp_L0():
                    if A.live:
                        exp_one("L0", A)

                def hT_hi_L1a():
                    if B.live:
                        act.wait_ge(sem("L1a_hT"), B.made())
                        act.wait_ge(sem("L1a_xl"), B.made(1))
                        activation(hT_hi[1][:], bank_b[:, 2, :], ACT.Copy).then_inc(sem("L1a_hT_hi"), 1)

                def pT_L0():
                    if A.live:
                        pT_one("L0", A, bank_a[:, 0:P])

                def hT_hi_L3():
                    if E.live:
                        act.wait_ge(sem("L3_hT"), E.made())
                        act.wait_ge(sem("L3_xl"), E.made(1))
                        activation(hT_hi[3][:], bank_e[:, 0, :], ACT.Copy).then_inc(sem("L3_hT_hi"), 1)

                def norm0():
                    if N0.live:
                        norm(0, N0, ("L0_out", 2))

                def norm1():
                    if A.live:
                        norm(1, A, ("L1a_hT", 1))

                def exp_L2():
                    if Dg.live:
                        exp_one("L2", Dg)

                def pT_L2():
                    if Dg.live:
                        pT_one("L2", Dg, bank_a[:, 0:P])

                def exp_L1a():
                    if B.live:
                        act.wait_ge(sem("L1a_shifted"), B.made())
                        act.wait_ge(sem("L1a_prob"), B.made(1))
                        activation(dB[:], dB[:], ACT.Exp, scale=-1.0).then_inc(sem("L1a_exp"), 1)

                def values_L3():
                    if E.live:
                        act.wait_ge(sem("st3_made"), E.made())
                        act.wait_ge(sem("L3_out"), E.made(1))
                        src = bank_e[:, :, 0:D // 2].rearrange("p b (k n) -> p b k n", k=HB)
                        activation(xa_heads[:, :, 0:K3].rearrange("p (b k) n -> p b k n", b=2), src, ACT.Copy)\
                            .then_inc(sem("xa_made"), 1)

                def exp_L1b():
                    if Cg.live:
                        exp_one("L1b", Cg)

                def pT_L1a():
                    if B.live:
                        act.wait_ge(sem("L1a_turned"), B.made())
                        act.wait_ge(sem("L1a_out1"), B.made(1))
                        activation(pTB[:], bank_b[:, 2, :].rearrange("p (k n) -> p k n", k=H1), ACT.Copy)\
                            .then_inc(sem("L1a_pT"), 1)

                def pT_L1b():
                    if Cg.live:
                        pT_one("L1b", Cg, bank_c[:, 0, 0:P])

                def norm3():
                    if Dg.live:
                        norm(3, Dg, ("L3_hT", 1))

                def elu_exp(i):
                    if B.live:
                        act.wait_ge(sem(f"L1a_out{i}"), B.made())
                        act.wait_ge(sem(("g_made_first", "g_made_last")[i]), B.made(1))
                        half = slice(i * (C1 // 2), (i + 1) * (C1 // 2))
                        activation(elu[:, half, :], bank_b[:, i, :].rearrange("p (c n) -> p c n", c=C1 // 2),
                                   ACT.Exp).then_inc(sem(f"elu_exp{i}"), 1)

                def g_high(i):
                    if B.live:
                        act.wait_ge(sem(("g_made_first", "g_made_last")[i]), B.made())
                        act.wait_ge(sem("L1b_xl"), B.made(1))
                        half = slice(i * (C1 // 2), (i + 1) * (C1 // 2))
                        activation(g_hi[:, half, :], g1[:, half, :], ACT.Copy).then_inc(sem(f"g_hi{i}"), 1)

                def exp3(i):
                    if Z.live:
                        act.wait_ge(sem(f"L3_shifted{i}"), Z.made())
                        act.wait_ge(sem(f"L3_turned{i}"), Z.made(1))
                        activation(pE[:, i * HB:(i + 1) * HB, :], nlE[:, i * HB:(i + 1) * HB, :], ACT.Exp,
                                   scale=-1.0).then_inc(sem(f"L3_exp{i}"), 1)

                hT_hi_L1a()
                exp_L0()
                norm2()
                exp3(0)
                exp3(1)
                pT_L0()
                norm0()
                pT_L3()
                hT_hi_L3()
                norm1()
                exp_L1a()
                exp_L2()
                values_L3()
                pT_L2()
                exp_L1b()
                pT_L1a()
                pT_L1b()
                elu_exp(0)
                elu_exp(1)
                g_high(0)
                g_high(1)
                norm3()

            run_turns(act, G, turn)

        @block.vector
        def _(dve):
            tt, ts, stt = nc.vector.tensor_tensor, nc.vector.tensor_scalar, nc.vector.scalar_tensor_tensor

            dve.wait_ge(sem("consts_in"), 16 * CONSTS)
            ts(nident[:], ident[:], -1.0, None, ALU.mult).then_inc(sem("setup_done"), 1)
            nc.vector.tensor_copy(identb[:], ident[:]).then_inc(sem("setup_done"), 1)
            ts(offdiag[:], ident[:], -1.0, 1.0, ALU.mult, ALU.add).then_inc(sem("setup_vec"), 1)
            nc.vector.memset(nhalf[:], -0.5).then_inc(sem("setup_vec"), 1)
            ts(att1[0][:, 0:D1], att1[0][:, 0:D1], -1.0, None, ALU.mult).then_inc(sem("setup_vec"), 1)
            ts(att2[0], att2[0], -1.0, None, ALU.mult).then_inc(sem("setup_vec"), 1)
            ts(att3[0], att3[0], -1.0, None, ALU.mult).then_inc(sem("setup_vec"), 1)
            ts(s_row[2][:], s_row[2][:], -1.0, None, ALU.mult).then_inc(sem("setup_vec"), 1)
            nc.vector.memset(b1_row[:, D1:E1], 0.0).then_inc(sem("setup_vec"), 1)
            nc.vector.memset(b2_row[:, D:E2], 0.0).then_inc(sem("setup_vec"), 1)
            nc.vector.memset(xa[:], 1.0).then_inc(sem("setup_done"), 1)
            dve.wait_ge(sem("u0_made"), 1)
            ts(s_row[0][:], bank_e[:, 0, :], -1.0, None, ALU.mult).then_inc(sem("setup_vec"), 1)
            nc.vector.tensor_copy(t_row[0][:], bank_e[:, 1, :]).then_inc(sem("setup_vec"), 1)
            dve.wait_ge(sem("setup_vec"), 10)

            his = 0
            for n, (kind, c) in enumerate(w_chunks):
                hi, lo, cols, (s_at, t_at), heads, att = w_parts(kind)
                width = w_cols[kind]
                dve.wait_ge(sem("w_in0" if n % 2 == 0 else "w_in1"), 16 * (n // 2 + 1))
                dve.wait_ge(sem("w_split"), n)
                for i in range(2):
                    if i or n:
                        dve.wait_ge(sem("ext_sums"), 2 * n + i)
                    tt(multiplied[:, 0:width], stage[n % 2][:, 0:width], att[i][:, 0:width], ALU.mult)\
                        .then_inc(sem("ext_products"), 1)
                    dve.wait_ge(sem("ext_products"), 2 * n + i + 1)
                    last = nc.vector.tensor_reduce(
                        ext[:, n % 2, 8 * i:8 * i + heads],
                        multiplied[:, 0:width].rearrange("p (h k) -> p h k", h=heads), AX_X, ALU.add)
                    last.then_inc(sem("ext_sums"), 1)
                dve.wait_ge(sem("ext_sums"), 2 * n + 2)
                nc.vector.tensor_copy(ext[:, n % 2, 8 + heads:10], ext[:, n % 2, 0:2 - heads])\
                    .then_inc(sem("ext_made"), 1) if heads < 2 else \
                    nc.vector.memset(nm1["L0"][:], 0.0).then_inc(sem("ext_made"), 1)
                his += len(cols) + 2 + (kind == "w2")
                dve.wait_ge(sem("w_hi"), his)
                dve.wait_ge(sem("ext_made"), n + 1)
                parts = [(to, stage[n % 2][:, frm:frm + count], count) for to, frm, count in cols]
                parts += [(s_at, ext[:, n % 2, 0:heads], heads), (t_at, ext[:, n % 2, 8:8 + heads], heads)]
                if kind == "w2":
                    parts.append((D + 2, hi[:, c, D + 2:E2].bitcast(F32), 2))
                for k, (to, whole, count) in enumerate(parts):
                    last = tt(lo[:, c, to:to + count], whole, hi[:, c, to:to + count].bitcast(F32), ALU.subtract)
                last.then_inc(sem("w_split"), 1)
            dve.wait_ge(sem("w_split"), len(w_chunks))

            def stats(layer, g, src):
                nc.vector.bn_stats(bn[layer][:], src).then_inc(sem(f"bn_made{layer}"), 1)
                dve.wait_ge(sem(f"bn_made{layer}"), g.made())
                dve.wait_ge(sem(f"rs_made{layer}"), g.made(1))
                dve.sem_inc(sem("passed_dve"), 1)
                nc.vector.bn_aggr(mv[layer][:], bn[layer][:]).then_inc(sem(f"mv_made{layer}"), 1)

            def score_columns(layer, g, scores):
                dve.wait_ge(sem(f"h_made{layer}"), g.made())
                dve.wait_ge(sem(scores), g.made(1))
                for i, (row, sign) in enumerate(((s_row, 1.0), (t_row, 1.0))):
                    last = nc.vector.tensor_tensor_reduce(product[:, layer + i, :], h[layer][:, g.slot(2) if layer == 0 else 0, :], row[layer][:], sign, 0.0,
                                                          ALU.mult, ALU.add, st[layer][:, i:i + 1])
                last.then_inc(sem(f"st_made{layer}"), 1)

            def softmax_one(key, g, bank, ns, bias=None):
                dve.wait_ge(sem(f"{key}_scores"), g.made())
                dve.wait_ge(sem(f"{key}_exp"), g.made(1))
                if bias is None:
                    ts(nl1[key][:, 0, :], bank, ns, None, ALU.add).then_inc(sem(f"{key}_v"), 1)
                else:
                    ts(nl1[key][:, 0, :], bank, ns, bias, ALU.add, ALU.subtract).then_inc(sem(f"{key}_v"), 1)
                dve.wait_ge(sem(f"{key}_v"), g.made())
                stt(nl1[key][:, 1, :], nl1[key][:, 0, :], SLOPE, nl1[key][:, 0, :], ALU.mult, ALU.min)\
                    .then_inc(sem(f"{key}_nl"), 1)
                dve.wait_ge(sem(f"{key}_nl"), g.made())
                nc.vector.tensor_reduce(nm1[key][:], nl1[key][:, 1, :], AX_X, ALU.min).then_inc(sem(f"{key}_min"), 1)

            def recip_one(key, g):
                dve.wait_ge(sem(f"{key}_exp"), g.made())
                nc.vector.reciprocal(sum1[key][:, 1:2], sum1[key][:, 0:1]).then_inc(sem(f"{key}_recip"), 1)

            def residual(key, g, bank, src, dst, made):
                dve.wait_ge(sem(f"{key}_out"), g.made())
                dve.wait_ge(sem(f"{key}_recip"), g.made())
                stt(dst, bank, sum1[key][:, 1:2], src, ALU.mult, ALU.add).then_inc(sem(made), 1)

            def turn(t):
                N0, A, B, Cg, Dg, E, Z = [t.graph(k) for k in range(7)]

                def stats_2():
                    if Cg.live:
                        dve.wait_ge(sem("x2_made"), Cg.made())
                        stats(2, Cg, x2[:])

                def min_L0():
                    if A.live:
                        softmax_one("L0", A, bank_a[:, 0:P], st[0][:, 0:1])

                def result_L3():
                    if Z.live:
                        dve.wait_ge(sem("L3_out"), Z.made())
                        wide = bank_e[:, :, 0:HB * KA].rearrange("p b (k n) -> p b k n", k=HB)
                        nc.vector.reciprocal(rcE[:], wide[:, :, :, K3]).then_inc(sem("L3_recip"), 1)
                        dve.wait_ge(sem("L3_recip"), Z.made())
                        dve.wait_ge(sem("out_made"), Z.made(1))
                        r4 = rE[:].rearrange("p (b k n) -> p b k n", b=2, k=HB)
                        rc4 = rcE[:].rearrange("p b (k a) -> p b k a", a=1).to_broadcast([P, 2, HB, K3])
                        tt(r4, wide[:, :, :, 0:K3], rc4, ALU.mult).then_inc(sem("out_read"), 1)

                def out_L3():
                    if Z.live:
                        dve.wait_ge(sem("out_read"), Z.made())
                        dve.wait_ge(sem(f"out_stored{Z.slot(OR)}"), Z.turns_of(OR, 16, OR))
                        stt(out_sb[:, Z.slot(OR), :], rE[:], 0.0, x3[:, Z.slot(X3R), :], ALU.max, ALU.add)\
                            .then_inc(sem("out_made"), 1)

                def columns_L2():
                    if Dg.live:
                        score_columns(2, Dg, "L2_scores")

                def hT_lo_L1a():
                    if B.live:
                        dve.wait_ge(sem("L1a_hT_hi"), B.made())
                        dve.wait_ge(sem("L1a_xl"), B.made(1))
                        tt(hT_lo[1][:], bank_b[:, 2, :], hT_hi[1][:].bitcast(F32), ALU.subtract)\
                            .then_inc(sem("L1a_hT_lo"), 1)

                def recip_L0():
                    if A.live:
                        recip_one("L0", A)

                def stats_0():
                    if N0.live:
                        dve.wait_ge(sem(f"x_loaded{N0.slot(XR)}"), N0.turns_of(XR, 32))
                        stats(0, N0, x_in[:, N0.slot(XR), :])

                def columns_L0():
                    if N0.live:
                        score_columns(0, N0, "L0_scores")

                def values_L1a():
                    if B.live:
                        dve.wait_ge(sem("L1a_xl"), B.made())
                        dve.wait_ge(sem("L1a_out1"), B.made(1))
                        tt(xl[:].rearrange("p (b n) -> p b n", b=3), bank_b[:, :, 0:B1],
                           b1_row[:].rearrange("p (b n) -> p b n", b=3), ALU.add).then_inc(sem("xl_made"), 1)

                def residual_L0():
                    if A.live:
                        dve.wait_ge(sem("h_made1"), A.made(3))
                        residual("L0", A, bank_a[:], x_in[:, A.slot(XR), :], x1[:, A.slot(X1R), :], "x1_made")

                def stats_1():
                    if A.live:
                        dve.wait_ge(sem("x1_made"), A.made())
                        stats(1, A, x1[:, A.slot(X1R), :])

                def hT_lo_L3():
                    if E.live:
                        dve.wait_ge(sem("L3_hT_hi"), E.made())
                        dve.wait_ge(sem("L3_xl"), E.made(1))
                        tt(hT_lo[3][:], bank_e[:, 0, :], hT_hi[3][:].bitcast(F32), ALU.subtract)\
                            .then_inc(sem("L3_hT_lo"), 1)

                def min_L1a():
                    if B.live:
                        dve.wait_ge(sem("L1a_scores"), B.made())
                        dve.wait_ge(sem("L1a_shifted"), B.made(1))
                        ns = xl[:, D1:D1 + H1].rearrange("p (h a) -> p h a", a=1).to_broadcast([P, H1, P])
                        tt(nlB[:, 0], bank_b[:, 2, :].rearrange("p (h n) -> p h n", h=H1), ns, ALU.add)\
                            .then_inc(sem("L1a_v"), 1)
                        dve.wait_ge(sem("L1a_v"), B.made())
                        stt(nlB[:, 1], nlB[:, 0], SLOPE, nlB[:, 0], ALU.mult, ALU.min).then_inc(sem("L1a_nl"), 1)
                        dve.wait_ge(sem("L1a_nl"), B.made())
                        nc.vector.tensor_reduce(nmB[:], nlB[:, 1], AX_X, ALU.min).then_inc(sem("L1a_min"), 1)

                def min_L2():
                    if Dg.live:
                        softmax_one("L2", Dg, bank_a[:, 0:P], st[2][:, 0:1], attn_b_all[:])

                def sum_L1a():
                    if B.live:
                        dve.wait_ge(sem("L1a_exp"), B.made())
                        dve.wait_ge(sem("L1a_prob"), B.made(1))
                        nc.vector.tensor_reduce(sumB[:, 0, :], dB[:], AX_X, ALU.add).then_inc(sem("L1a_sum"), 1)
                        dve.wait_ge(sem("L1a_sum"), B.made())
                        nc.vector.reciprocal(sumB[:, 1, :], sumB[:, 0, :]).then_inc(sem("L1a_recip"), 1)

                def recip_L2():
                    if Dg.live:
                        recip_one("L2", Dg)

                def values_L1b():
                    if Cg.live:
                        dve.wait_ge(sem("L1b_xl"), Cg.made())
                        dve.wait_ge(sem("L1b_out"), Cg.made(1))
                        tt(xl2[:].rearrange("p (b n) -> p b n", b=2), bank_c[:, :, 0:B2],
                           b2_row[:].rearrange("p (b n) -> p b n", b=2), ALU.add).then_inc(sem("xl2_made"), 1)

                def columns_L3():
                    if E.live:
                        dve.wait_ge(sem("L3_xl"), E.made())
                        dve.wait_ge(sem("L3_scores1"), E.made(1))
                        tt(st3[:, 0, :], bank_e[:, 0, D // 2:B3], b_att_all[:], ALU.subtract).then_inc(sem("st3_s"), 1)
                        nc.vector.tensor_copy(st3[:, 1, :], bank_e[:, 1, D // 2:B3]).then_inc(sem("st3_made"), 1)

                def residual_L2():
                    if Dg.live:
                        dve.wait_ge(sem("out_made"), Dg.made(2))
                        residual("L2", Dg, bank_a[:], x2[:], x3[:, Dg.slot(X3R), :], "x3_made")

                def stats_3():
                    if Dg.live:
                        dve.wait_ge(sem("x3_made"), Dg.made())
                        stats(3, Dg, x3[:, Dg.slot(X3R), :])

                def min_L1b():
                    if Cg.live:
                        softmax_one("L1b", Cg, bank_c[:, 0, 0:P], xl2[:, D:D + 1])

                def v_L3(i):
                    if E.live:
                        dve.wait_ge(sem(f"L3_scores{i}"), E.made())
                        dve.wait_ge(sem("L3_exp1"), E.made(1))
                        dve.wait_ge(sem("st3_s"), E.made())
                        half = slice(i * HB, (i + 1) * HB)
                        ns = st3[:, 0, half].rearrange("p (h a) -> p h a", a=1).to_broadcast([P, HB, P])
                        tt(nlE[:, half, :], bank_e[:, i, :].rearrange("p (h n) -> p h n", h=HB), ns, ALU.add)\
                            .then_inc(sem(f"L3_v{i}"), 1)

                def recip_L1b():
                    if Cg.live:
                        recip_one("L1b", Cg)

                def nl_L3():
                    if Z.live:
                        dve.wait_ge(sem("L3_v1"), Z.made())
                        stt(nlE[:], nlE[:], SLOPE, nlE[:], ALU.mult, ALU.min).then_inc(sem("L3_nl"), 1)

                def min_L3():
                    if Z.live:
                        dve.wait_ge(sem("L3_nl"), Z.made())
                        nc.vector.tensor_reduce(nmE[:], nlE[:], AX_X, ALU.min).then_inc(sem("L3_min"), 1)

                def elu_L1a(i, name):
                    if B.live:
                        half = slice(i * (C1 // 2), (i + 1) * (C1 // 2))
                        dve.wait_ge(sem(f"elu_exp{i}"), B.made())
                        ts(elu[:, half, :], elu[:, half, :], 1.0, -1.0, ALU.min, ALU.add)\
                            .then_inc(sem(f"elu_clamped{i}"), 1)
                        dve.wait_ge(sem(f"elu_clamped{i}"), B.made())
                        dve.wait_ge(sem("g_lo_last"), B.made(1))
                        tt(g1[:, half, :], bank_b[:, i, :].rearrange("p (c n) -> p c n", c=C1 // 2),
                           elu[:, half, :], ALU.max).then_inc(sem(name), 1)

                def g_lo_first():
                    if B.live:
                        dve.wait_ge(sem("g_hi0"), B.made())
                        half = slice(0, C1 // 2)
                        tt(g_lo[:, half, :], g1[:, half, :], g_hi[:, half, :].bitcast(F32), ALU.subtract)\
                            .then_inc(sem("g_lo_first"), 1)

                def residual_L1b():
                    if Cg.live:
                        dve.wait_ge(sem("h_made2"), Cg.made(1))
                        residual("L1b", Cg, bank_c[:, 1, :], x1[:, Cg.slot(X1R), :], x2[:], "x2_made")

                hT_lo_L1a()
                min_L0()
                nl_L3()
                min_L3()
                stats_0()
                recip_L0()
                columns_L2()
                values_L1a()
                residual_L0()
                result_L3()
                stats_1()
                out_L3()
                min_L1a()
                hT_lo_L3()
                values_L1b()
                min_L2()
                sum_L1a()
                columns_L3()
                recip_L2()
                min_L1b()
                v_L3(0)
                columns_L0()
                residual_L2()
                stats_3()
                recip_L1b()
                elu_L1a(0, "g_made_first")
                elu_L1a(1, "g_made_last")
                residual_L1b()
                g_lo_first()
                v_L3(1)
                stats_2()

            run_turns(dve, G, turn)

        @block.gpsimd
        def _(pool):
            tt, ts = nc.gpsimd.tensor_tensor, nc.gpsimd.tensor_scalar
            pool.wait_ge(sem("setup_vec"), 10)
            pool.wait_ge(sem("w_split"), len(w_chunks))

            def scale_and_bias(layer, g):
                pool.wait_ge(sem(f"mv_made{layer}"), g.made())
                pool.wait_ge(sem(f"h_made{layer}"), g.made(1))
                pool.sem_inc(sem("passed_pool"), 1)
                v, r, b = [rs[layer][:, k:k + 1] for k in range(3)]
                ts(v, mv[layer][:, 1:2], EPS, None, ALU.add).then_inc(sem(f"var_made{layer}"), 1)
                pool.wait_ge(sem(f"var_made{layer}"), g.made())
                tt(r, v, nhalf[:], ALU.pow).then_inc(sem(f"rstd_made{layer}"), 1)
                pool.wait_ge(sem(f"rstd_made{layer}"), g.made())
                pool.sem_inc(sem("passed_pool"), 1)
                ts(b, mv[layer][:, 0:1], r, -1.0, ALU.mult, ALU.mult).then_inc(sem(f"rs_made{layer}"), 1)

            def turn(t):
                N0, A, B, Cg, Dg, E, Z = [t.graph(k) for k in range(7)]

                def norm_2():
                    if Dg.live:
                        scale_and_bias(2, Dg)

                def norm_0_masks():
                    if N0.live:
                        scale_and_bias(0, N0)
                        s, m = N0.slot(XR), N0.slot(MR)
                        pool.wait_ge(sem(f"x_loaded{s}"), N0.turns_of(XR, 32))
                        pool.wait_ge(sem("L3_scores1"), N0.made(MR))
                        pool.sem_inc(sem("passed_pool"), 1)
                        ts(mask[:, m, :], adj_in[:, s, :], -BIG, BIG, ALU.mult, ALU.add).then_inc(sem("mask_made"), 1)
                        pool.wait_ge(sem("mask_made"), N0.made())
                        tt(mask_loop[:, m, :], mask[:, m, :], offdiag[:], ALU.mult).then_inc(sem("masks_made"), 1)

                def norm_1():
                    if A.live:
                        scale_and_bias(1, A)

                def shift_L1a():
                    if B.live:
                        pool.wait_ge(sem("L1a_min"), B.made())
                        pool.wait_ge(sem("L1a_prob"), B.made(1))
                        nm = nmB[:].rearrange("p (h a) -> p h a", a=1).to_broadcast([P, H1, P])
                        tt(dB[:], nlB[:, 1], nm, ALU.subtract).then_inc(sem("L1a_shifted"), 1)
                        pool.wait_ge(sem("L1a_recip"), B.made())
                        pool.wait_ge(sem("L1a_turned"), B.made(1))
                        rc = sumB[:, 1, :].rearrange("p (h a) -> p h a", a=1).to_broadcast([P, H1, P])
                        tt(pB[:], dB[:], rc, ALU.mult).then_inc(sem("L1a_prob"), 1)

                def norm_3():
                    if Dg.live:
                        scale_and_bias(3, Dg)

                def shift_L3():
                    if Z.live:
                        for i in range(2):
                            half = slice(i * HB, (i + 1) * HB)
                            pool.wait_ge(sem("L3_min"), Z.made())
                            nm = nmE[:, half].rearrange("p (h a) -> p h a", a=1).to_broadcast([P, HB, P])
                            tt(nlE[:, half, :], nlE[:, half, :], nm, ALU.subtract).then_inc(sem(f"L3_shifted{i}"), 1)

                def g_lo_last():
                    if B.live:
                        pool.wait_ge(sem("g_hi1"), B.made())
                        pool.wait_ge(sem("L1b_xl"), B.made(1))
                        half = slice(C1 // 2, C1)
                        tt(g_lo[:, half, :], g1[:, half, :], g_hi[:, half, :].bitcast(F32), ALU.subtract)\
                            .then_inc(sem("g_lo_last"), 1)

                norm_2()
                shift_L3()
                norm_0_masks()
                norm_1()
                shift_L1a()
                norm_3()
                g_lo_last()

            run_turns(pool, G, turn)


CONSTS = 19

_INS = ["x", "adj", "L0_gnn_W", "L0_gnn_a1", "L0_gnn_a2", "L1_gnn_W1", "L1_gnn_att_src1", "L1_gnn_att_dst1",
        "L1_gnn_b1", "L1_gnn_W2", "L1_gnn_att_src2", "L1_gnn_att_dst2", "L1_gnn_b2", "L2_gnn_attn_w_src",
        "L2_gnn_attn_w_dst", "L2_gnn_attn_b", "L3_gnn_W_proj", "L3_gnn_W_att", "L3_gnn_b_att"]


def kernel(**inputs):
    import concourse.bacc as bacc
    import numpy as np
    from concourse.bass_utils import run_bass_kernel_spmd

    nc = bacc.Bacc("TRN2", target_bir_lowering=False, num_devices=1)
    ins = {f"in_{name}": np.ascontiguousarray(inputs[name]) for name in _INS}
    ins["in_ident"] = np.eye(P, dtype=np.float32)
    aps = [nc.dram_tensor(n, a.shape, mybir.dt.from_np(a.dtype), kind="ExternalInput").ap() for n, a in ins.items()]
    out = nc.dram_tensor("out", inputs["x"].shape, F32, kind="ExternalOutput").ap()
    build(nc, *aps, out)
    r = run_bass_kernel_spmd(nc, [ins], core_ids=[0])
    return r.results[0]["out"]
```

```python
from contextlib import ExitStack

import concourse.bass as bass
from concourse import mybir

ALU = mybir.AluOpType
ACT = mybir.ActivationFunctionType
AX_X = mybir.AxisListType.X
F32 = mybir.dt.float32
F32R = mybir.dt.float32r
BF16 = mybir.dt.bfloat16
I32 = mybir.dt.int32

P = 128
SKEW = 6
UNROLL = 6
PEELED = SKEW + 2
SLOPE = 0.2
BIG = 5.0e9
EPS = 1e-5


class Graph:

    def __init__(self, turn, skew):
        self.turn, self.skew = turn, skew
        self.offset = turn.step - skew

    @property
    def live(self):
        return self.turn.loop is not None or 0 <= self.offset < self.turn.graphs

    def slot(self, ring):
        return self.offset % ring

    def made(self, back=0):
        return self.turn.value(UNROLL, self.offset + 1 - back)

    def turns_of(self, ring, each, back=0):
        return self.turn.value(UNROLL // ring * each, ((self.offset - back) // ring + 1) * each)

    def index(self):
        return self.turn.value(UNROLL, self.offset)


class Turn:
    def __init__(self, eng, graphs, step, loop=None, kept=None):
        self.eng, self.graphs, self.step, self.loop, self.kept = eng, graphs, step, loop, kept

    def graph(self, skew):
        return Graph(self, skew)

    def value(self, scale, add):
        if self.loop is None:
            return max(0, add)
        if (scale, add) not in self.kept:
            self.kept[scale, add] = self.eng.snap(self.loop * scale + add)
        return self.kept[scale, add]


def run_turns(eng, graphs, turn_body):
    turns = graphs + SKEW
    loops = (graphs - PEELED) // UNROLL
    for n in range(PEELED):
        turn_body(Turn(eng, graphs, n))
    if loops > 1:
        with eng.Fori(0, loops) as loop:
            kept = {}
            for j in range(UNROLL):
                turn_body(Turn(eng, graphs, PEELED + j, loop, kept))
    else:
        loops = 0
    for n in range(PEELED + loops * UNROLL, turns):
        turn_body(Turn(eng, graphs, n))


def build(nc, x, adj, a0_w, a0_a1, a0_a2, w1, att_src1, att_dst1, b1, w2, att_src2, att_dst2, b2,
          attn_src, attn_dst, attn_b, w_proj, w_att, b_att, ident_in, out):
    G, N, D = x.shape
    H1, F1 = att_src1.shape
    D1 = H1 * F1
    H3 = w_att.shape[0]
    K3 = w_att.shape[1] // 2
    assert N == P and D == 512 and D1 % P == 0 and H3 * K3 == D
    C = D // P
    C1 = D1 // P
    E1 = D1 + 2 * H1
    B1 = E1 // 3
    E2 = D + 4
    B2 = E2 // 2
    B3 = D // 2 + H3
    HB = H3 // 2
    KA = K3 + 1
    NMIN = 96
    assert E1 % 6 == 0 and B1 <= 512

    with ExitStack() as ctx:
        def sb(name, shape, dt=F32):
            return ctx.enter_context(nc.sbuf_tensor(name, shape, dt))

        def psum(name, shape):
            return ctx.enter_context(nc.psum_tensor(name, shape, F32))

        sems = {}

        def sem(name):
            if name not in sems:
                sems[name] = ctx.enter_context(nc.semaphore(name))
            return sems[name]

        ident = sb("ident", [P, P])
        nident = sb("nident", [P, P])
        identb = sb("identb", [P, P], BF16)
        offdiag = sb("offdiag", [P, P], BF16)
        nhalf = sb("nhalf", [P, 1])
        w1_hi = sb("w1_hi", [P, C, E1], F32R)
        w1_lo = sb("w1_lo", [P, C, E1], F32R)
        w2_hi = sb("w2_hi", [P, C1, E2], F32R)
        w2_lo = sb("w2_lo", [P, C1, E2], F32R)
        w3_hi = sb("w3_hi", [P, C, 2 * B3], F32R)
        w3_lo = sb("w3_lo", [P, C, 2 * B3], F32R)
        b1_row = sb("b1_row", [P, E1])
        b2_row = sb("b2_row", [P, E2])
        s_row = {0: sb("s_row0", [P, D]), 2: sb("s_row2", [P, D])}
        t_row = {0: sb("t_row0", [P, D]), 2: sb("t_row2", [P, D])}
        attn_b_all = sb("attn_b_all", [P, 1])
        b_att_all = sb("b_att_all", [P, H3])

        XR, MR, X1R, X3R, OR = 3, 6, 3, 2, 2
        x_in = sb("x_in", [P, XR, D])
        adj_in = sb("adj_in", [P, XR, P], I32)
        mask = sb("mask", [P, MR, P], BF16)
        mask_loop = sb("mask_loop", [P, MR, P], BF16)
        x1 = sb("x1", [P, X1R, D])
        x2 = sb("x2", [P, D])
        x3 = sb("x3", [P, X3R, D])
        out_sb = sb("out_sb", [P, OR, D])

        h = [sb(f"h{i}", [P, 1, D]) for i in range(4)]
        bn = [sb(f"bn{i}", [P, 6]) for i in range(4)]
        mv = [sb(f"mv{i}", [P, 2]) for i in range(4)]
        rs = [sb(f"rs{i}", [P, 3]) for i in range(4)]
        st = {i: sb(f"st{i}", [P, 2]) for i in (0, 2)}
        product = sb("product", [P, 4, D], BF16)
        one = ("L0", "L1b", "L2")
        nl1 = {k: sb(f"nl_{k}", [P, P]) for k in one}
        nm1 = {k: sb(f"nm_{k}", [P, 1]) for k in one}
        p1 = {k: sb(f"p_{k}", [P, P]) for k in one}
        pT_hi = {k: sb(f"pT_hi_{k}", [P, P], F32R) for k in one}
        pT_lo = {k: sb(f"pT_lo_{k}", [P, P], F32R) for k in one}
        v_hi = {k: sb(f"v_hi_{k}", [P, D], F32R) for k in one}
        v_lo = {k: sb(f"v_lo_{k}", [P, D], F32R) for k in one}
        sum1 = {k: sb(f"sum_{k}", [P, 2]) for k in one}
        hT_hi = {k: sb(f"hT_hi{k}", [P, D], F32R) for k in (1, 3)}
        hT_lo = {k: sb(f"hT_lo{k}", [P, D], F32R) for k in (1, 3)}
        xl = sb("xl", [P, E1])
        nlB = sb("nlB", [P, H1, P])
        nmB = sb("nmB", [P, H1])
        dB = sb("dB", [P, H1, P])
        sumB = sb("sumB", [P, 2, H1])
        pTB = sb("pTB", [P, H1, P])
        elu = sb("elu", [P, C1, P])
        g1 = sb("g1", [P, C1, P])
        g_hi = sb("g_hi", [P, C1, P], F32R)
        g_lo = sb("g_lo", [P, C1, P], F32R)
        xl2 = sb("xl2", [P, E2])
        xa = sb("xa", [P, H3 * KA + NMIN - KA])
        st3 = sb("st3", [P, 2, H3])
        t3_hi, t3_lo = sb("t3_hi", [P, HB], F32R), sb("t3_lo", [P, HB])
        one_col, ones_r = sb("one_col", [P, 1]), sb("ones_r", [P, 1], F32R)
        nlE = sb("nlE", [P, H3, P])
        nmE = sb("nmE", [P, H3])
        pE = sb("pE", [P, H3, P])
        pTE = sb("pTE", [P, H3, P])
        rcE = sb("rcE", [P, 2, HB])
        rE = sb("rE", [P, D])

        bank_a = psum("bank_a", [P, 512])
        bank_b = psum("bank_b", [P, 3, 512])
        bank_c = psum("bank_c", [P, 2, 512])
        bank_e = psum("bank_e", [P, 2, 512])

        g_hi_all = g_hi[:].rearrange("p c n -> p (c n)")
        g_lo_all = g_lo[:].rearrange("p c n -> p (c n)")
        diag_hi, diag_lo = [part[1][:].rearrange("p (h n) -> p h n", h=HB) for part in (hT_hi, hT_lo)]
        xa_heads = xa[:, 0:H3 * KA].rearrange("p (h k) -> p h k", h=H3)

        stage = [xl[:, 0:D1], elu[:].rearrange("p c n -> p (c n)"),
                 nlE[:].rearrange("p h n -> p (h n)"), g1[:].rearrange("p c n -> p (c n)")]
        ext = sb("ext", [P, 4, 16])
        att1 = [pE[:].rearrange("p h n -> p (h n)"), pTE[:].rearrange("p h n -> p (h n)")]
        att2 = [h[2][:, 0, :], h[3][:, 0, :]]
        stage3 = [nlE[:, 0:HB, :], nlE[:, HB:H3, :], pE[:, 0:HB, :], pE[:, HB:H3, :]]
        stage3 = [s.rearrange("p h n -> p (h n)") for s in stage3]
        att3 = [pTE[:, i * HB:(i + 1) * HB, :].rearrange("p h n -> p (h n)") for i in range(2)]
        scratch = product[:].rearrange("p a n -> p (a n)")
        WR = len(stage)
        w_chunks = [("w1", c) for c in range(C)] + [("w2", c) for c in range(C1)] + [("w3", c) for c in range(C)]
        prepared = {0: range(0, C), 1: range(C, C + C1), 2: range(C + C1, C + C1 + C // 2),
                    3: range(C + C1 + C // 2, len(w_chunks))}
        staged = [stage[n % WR] if n < C + C1 else stage3[n - C - C1] for n in range(len(w_chunks))]

        block = ctx.enter_context(nc.Block())

        def w_parts(kind, c, n):
            def two(w, lo, hi):
                return w.rearrange("p (b n) -> p b n", b=2)[:, :, lo:hi]
            e, src = ext[:, n % WR, :], staged[n]
            if kind == "w1":
                return ((w1_hi[:, c, 0:D1], w1_lo[:, c, 0:D1], src[:, 0:D1]),
                        (w1_hi[:, c, D1:E1], w1_lo[:, c, D1:E1], e[:, 0:2 * H1]))
            if kind == "w2":
                return ((w2_hi[:, c, 0:D], w2_lo[:, c, 0:D], src[:, 0:D]),
                        (w2_hi[:, c, D:E2], w2_lo[:, c, D:E2], e[:, 8:12]))
            return ((two(w3_hi[:, c, :], 0, D // 2), two(w3_lo[:, c, :], 0, D // 2), two(src[:, 0:D], 0, D // 2)),
                    (two(w3_hi[:, c, :], D // 2, B3), two(w3_lo[:, c, :], D // 2, B3), two(e[:, 0:2 * H3], 0, H3)))

        w_dram = {"w1": w1.rearrange("(c p) n -> c p n", p=P), "w2": w2.rearrange("(c p) n -> c p n", p=P),
                  "w3": w_proj.rearrange("(c p) n -> c p n", p=P)}
        w_cols = {"w1": D1, "w2": D, "w3": D}
        w_att_of = {"w1": (H1, att1, 0), "w2": (1, att2, 8), "w3": (H3, att3, 0)}

        @block.sync
        def _(sp):
            def row(src):
                return src.rearrange("(a n) -> a n", a=1)

            def spread(dst, src, name):
                sp.dma_start(dst, src.to_broadcast([P, src.shape[1]])).then_inc(sem(name), 16)

            def stage_weights(chunks):
                for n in chunks:
                    kind, c = w_chunks[n]
                    if kind == "w2":
                        sp.wait_ge(sem("w_split"), n - WR + 1)
                    if kind == "w3":
                        sp.wait_ge(sem("w_split"), C + C1)
                    if n == C + C1:
                        for i in range(2):
                            src = w_att[:, i * K3:(i + 1) * K3].rearrange("(a h) k -> a h k", a=1)
                            sp.dma_start(att3[i].rearrange("p (h k) -> p h k", h=H3),
                                         src.to_broadcast([P, H3, K3])).then_inc(sem("att3_in"), 16)
                    sp.dma_start(staged[n][:, 0:w_cols[kind]], w_dram[kind][c])\
                        .then_inc(sem(f"w_in{n % WR}"), 16)

            spread(att1[1][:, 0:D1], row(att_src1.rearrange("h f -> (h f)")), "att1_in")
            spread(att1[0][:, 0:D1], row(att_dst1.rearrange("h f -> (h f)")), "att1_in")
            stage_weights(range(0, 1))
            sp.dma_start(st3[:, 0, 0:C], a0_a1.rearrange("(p c) a -> p (c a)", p=P)).then_inc(sem("a0_in"), 16)
            sp.dma_start(st3[:, 1, 0:C], a0_a2.rearrange("(p c) a -> p (c a)", p=P)).then_inc(sem("a0_in"), 16)
            for c in range(C):
                dst = (x3[:, c, :] if c < 2 else out_sb[:, c - 2, :])
                sp.dma_start(dst, a0_w.rearrange("(p c) f -> c p f", p=P)[c]).then_inc(sem("a0_in"), 16)
            sp.dma_start(ident[:], ident_in).then_inc(sem("ident_loaded"), 16)
            stage_weights(range(1, C))

            def load_rest():
                spread(att2[1], att_src2, "att2_in")
                spread(att2[0], att_dst2, "att2_in")
                for dst, src in ((b1_row[:, 0:D1], row(b1)), (b2_row[:, 0:D], row(b2)),
                                 (s_row[2][:], row(attn_src)), (t_row[2][:], row(attn_dst)),
                                 (attn_b_all[:], row(attn_b)), (b_att_all[:], row(b_att))):
                    spread(dst, src, "rows_in")

            def load(g):
                s = g.slot(XR)
                sp.wait_ge(sem("x1_made"), g.made(XR))
                sp.wait_ge(sem("mask_made"), g.made(XR))
                sp.dma_start(x_in[:, s, :], x[g.index()]).then_inc(sem(f"x_loaded{s}"), 16)
                sp.dma_start(adj_in[:, s, :], adj[g.index()]).then_inc(sem(f"x_loaded{s}"), 16)

            def store(g):
                s = g.slot(OR)
                sp.wait_ge(sem("out_made"), g.made())
                sp.dma_start(out[g.index()], out_sb[:, s, :]).then_inc(sem(f"out_stored{s}"), 16)

            def turn(t):
                if t.graph(0).live:
                    load(t.graph(0))
                if t.graph(6).live:
                    store(t.graph(6))
                if t.loop is None and t.step == 0:
                    load_rest()
                if t.loop is None and t.step in (1, 2, 3):
                    stage_weights(prepared[t.step])

            run_turns(sp, G, turn)
            for s in range(OR):
                sp.wait_ge(sem(f"out_stored{s}"), 16 * len(range(s, G, OR)))

        @block.tensor
        def _(pe):
            mm = nc.tensor.matmul

            pe.wait_ge(sem("a0_in"), 16 * (2 + C))
            for i in range(2):
                for c in range(C):
                    w = x3[:, c, :] if c < 2 else out_sb[:, c - 2, :]
                    last = mm(bank_e[:, i, :], st3[:, i, c:c + 1].to_broadcast([P, P]), w,
                              start=(c == 0), stop=(c == C - 1))
            last.then_inc(sem("u0_made"), 1)
            pe.wait_ge(sem("setup_pe"), 4)

            def masks_and_t(bank, mask_l, mask_r, t_cols):
                heads = len(t_cols)
                mm(bank[:, 0:heads * P], mask_l, mask_r, start=True, stop=False)
                for k, t_col in enumerate(t_cols):
                    last = mm(bank[:, k * P:(k + 1) * P], t_col.to_broadcast([P, P]), nident[:],
                              start=False, stop=(k == heads - 1))
                return last

            def direct(m, heads):
                if heads == 1:
                    return identb[:], m
                return identb[:], m.rearrange("p (a n) -> p a n", a=1).to_broadcast([P, heads, P])

            def turned(m, heads):
                if heads == 1:
                    return m, identb[:]
                return m, identb[:].rearrange("p (a n) -> p a n", a=1).to_broadcast([P, heads, P])

            def to_columns(bank, src):
                for c in range(C):
                    last = nc.tensor.transpose(bank[:, c * P:(c + 1) * P], src[:, c * P:(c + 1) * P], ident[:])
                return last

            def project(banks, width, chunks, products, first, final):
                for c in chunks:
                    for n, (a, w) in enumerate(products):
                        for b, bank in banks.items():
                            last = mm(bank[:, 0:width], a[:, c * P:(c + 1) * P], w[:, c, b * width:(b + 1) * width],
                                      start=(first and c == chunks[0] and n == 0),
                                      stop=(final and c == chunks[-1] and n == len(products) - 1))
                return last

            def product_one(key, g, bank):
                pe.wait_ge(sem(f"{key}_v_lo"), g.made())
                pe.wait_ge(sem(f"{key}_pT_hi"), g.made())
                pe.wait_ge(sem(f"{key}_pT_lo"), g.made())
                mm(bank, pT_hi[key][:], v_hi[key][:], start=True, stop=False)
                mm(bank, pT_hi[key][:], v_lo[key][:], start=False, stop=False)
                mm(bank, pT_lo[key][:], v_hi[key][:], start=False, stop=True).then_inc(sem(f"{key}_out"), 1)

            def turn(t):
                A, B, Cg, Dg, E, Z = [t.graph(k) for k in (1, 2, 3, 4, 5, 6)]

                def turn_exp_L3():
                    if Z.live:
                        for i in range(2):
                            pe.wait_ge(sem(f"L3_exp{i}"), Z.made())
                            for k in range(HB):
                                head = i * HB + k
                                last = nc.tensor.transpose(bank_e[:, i, k * P:(k + 1) * P], pE[:, head, :], ident[:])
                            last.then_inc(sem(f"L3_turned{i}"), 1)

                def scores_L0():
                    if A.live:
                        pe.wait_ge(sem("st_made0"), A.made())
                        pe.wait_ge(sem("masks_made"), A.made())
                        if t.loop is None:
                            pe.wait_ge(sem("x1_made"), A.made(1))
                        pe.wait_ge(sem("x3_made"), A.made(4))
                        m_l, m_r = direct(mask[:, A.slot(MR), :], 1)
                        masks_and_t(bank_a, m_l, m_r, [st[0][:, 1:2]]).then_inc(sem("L0_scores"), 1)

                def product_L3():
                    if Z.live:
                        for i in range(2):
                            pe.wait_ge(sem(f"L3_pT{i}"), Z.made())
                            for k in range(HB):
                                head = i * HB + k
                                last = mm(bank_e[:, i, k * KA:k * KA + NMIN], pTE[:, head, :],
                                          xa[:, head * KA:head * KA + NMIN], start=True, stop=True)
                        last.then_inc(sem("L3_out"), 1)

                def turn_h1():
                    if B.live:
                        pe.wait_ge(sem("h_made1"), B.made())
                        pe.wait_ge(sem("L1a_pT"), B.made(1))
                        to_columns(bank_b[:, 2, :], h[1][:, 0, :]).then_inc(sem("L1a_hT"), 1)

                def turn_exp_L0():
                    if A.live:
                        pe.wait_ge(sem("L0_exp"), A.made())
                        nc.tensor.transpose(bank_a[:, 0:P], p1["L0"][:], ident[:]).then_inc(sem("L0_turned"), 1)

                def project_L1b_first():
                    if Cg.live:
                        if t.loop is None and t.step == 3:
                            pe.wait_ge(sem("w_split"), C + C1)
                        pe.wait_ge(sem("g_hi0"), Cg.made())
                        pe.wait_ge(sem("x2_made"), Cg.made(1))
                        banks, chunks = {0: bank_c[:, 0, :], 1: bank_c[:, 1, :]}, range(C1 // 2)
                        project(banks, B2, chunks, ((g_hi_all, w2_hi), (g_hi_all, w2_lo)), True, False)
                        pe.wait_ge(sem("g_lo_first"), Cg.made())
                        project(banks, B2, chunks, ((g_lo_all, w2_hi),), False, False)

                def project_L1a():
                    if B.live:
                        if t.loop is None and t.step == 2:
                            pe.wait_ge(sem("w_split"), C)
                        pe.wait_ge(sem("L1a_hT_hi"), B.made())
                        pe.wait_ge(sem("g_made_last"), B.made(1))
                        two, last = {0: bank_b[:, 0, :], 1: bank_b[:, 1, :]}, {2: bank_b[:, 2, :]}
                        high = ((hT_hi[1], w1_hi), (hT_hi[1], w1_lo))
                        low = ((hT_lo[1], w1_hi),)
                        project(two, B1, range(C), high, True, False)
                        pe.wait_ge(sem("L1a_hT_lo"), B.made())
                        project(two, B1, range(C), low, False, True)
                        project(last, B1, range(C), high + low, True, True).then_inc(sem("L1a_xl"), 1)

                def product_L0():
                    if A.live:
                        product_one("L0", A, bank_a[:])

                def turn_h3():
                    if E.live:
                        pe.wait_ge(sem("h_made3"), E.made())
                        pe.wait_ge(sem("out_read"), E.made(1))
                        to_columns(bank_e[:, 0, :], h[3][:, 0, :]).then_inc(sem("L3_hT"), 1)

                def scores_L1a():
                    if B.live:
                        pe.wait_ge(sem("xl_made"), B.made())
                        m_l, m_r = turned(mask_loop[:, B.slot(MR), :], H1)
                        masks_and_t(bank_b[:, 2, :], m_l, m_r,
                                    [xl[:, D1 + H1 + k:D1 + H1 + k + 1] for k in range(H1)]).then_inc(sem("L1a_scores"), 1)

                def scores_L2():
                    if Dg.live:
                        pe.wait_ge(sem("st_made2"), Dg.made())
                        if A.live:
                            pe.wait_ge(sem("x1_made"), A.made())
                        else:
                            pe.wait_ge(sem("x3_made"), Dg.made(1))
                        m_l, m_r = direct(mask_loop[:, Dg.slot(MR), :], 1)
                        masks_and_t(bank_a, m_l, m_r, [st[2][:, 1:2]]).then_inc(sem("L2_scores"), 1)

                def project_L1b_last():
                    if Cg.live:
                        pe.wait_ge(sem("g_hi1"), Cg.made())
                        pe.wait_ge(sem("g_lo_last"), Cg.made())
                        project({0: bank_c[:, 0, :], 1: bank_c[:, 1, :]}, B2, range(C1 // 2, C1),
                                ((g_hi_all, w2_hi), (g_hi_all, w2_lo), (g_lo_all, w2_hi)), False, True)\
                            .then_inc(sem("L1b_xl"), 1)

                def project_L3():
                    if E.live:
                        if t.loop is None and t.step == 5:
                            pe.wait_ge(sem("w_split"), len(w_chunks))
                        pe.wait_ge(sem("L3_hT_hi"), E.made())
                        high = ((hT_hi[3], w3_hi), (hT_hi[3], w3_lo))
                        low = ((hT_lo[3], w3_hi),)
                        project({1: bank_e[:, 1, :]}, B3, range(C), high, True, False)
                        pe.wait_ge(sem("L3_hT_lo"), E.made())
                        project({1: bank_e[:, 1, :]}, B3, range(C), low, False, True)
                        project({0: bank_e[:, 0, :]}, B3, range(C), high + low, True, True).then_inc(sem("L3_xl"), 1)

                def turn_exp_L2():
                    if Dg.live:
                        pe.wait_ge(sem("L2_exp"), Dg.made())
                        nc.tensor.transpose(bank_a[:, 0:P], p1["L2"][:], ident[:]).then_inc(sem("L2_turned"), 1)

                def scores_L1b():
                    if Cg.live:
                        pe.wait_ge(sem("xl2_made"), Cg.made())
                        m_l, m_r = turned(mask_loop[:, Cg.slot(MR), :], 1)
                        masks_and_t(bank_c[:, 0, :], m_l, m_r, [xl2[:, D + 1:D + 2]]).then_inc(sem("L1b_scores"), 1)

                def product_L2():
                    if Dg.live:
                        product_one("L2", Dg, bank_a[:])

                def scores3(i):
                    if E.live:
                        pe.wait_ge(sem("xa_made"), E.made())
                        m_l, m_r = direct(mask[:, E.slot(MR), :], HB)
                        if i == 0:
                            masks_and_t(bank_e[:, i, :], m_l, m_r, [st3[:, 1, k:k + 1] for k in range(HB)])\
                                .then_inc(sem("L3_scores0"), 1)
                        else:
                            pe.wait_ge(sem("L3_diag"), E.made())
                            ones = ones_r[:].to_broadcast([P, P])
                            mm(bank_e[:, i, :], m_l, m_r, start=True, stop=False)
                            mm(bank_e[:, i, :], ones, diag_hi, start=False, stop=False)
                            mm(bank_e[:, i, :], ones, diag_lo, start=False, stop=True).then_inc(sem("L3_scores1"), 1)

                def turn_prob_L1a():
                    if B.live:
                        pe.wait_ge(sem("L1a_prob"), B.made())
                        for k in range(H1):
                            last = nc.tensor.transpose(bank_b[:, 2, k * P:(k + 1) * P], dB[:, k, :], ident[:])
                        last.then_inc(sem("L1a_turned"), 1)

                def turn_exp_L1b():
                    if Cg.live:
                        pe.wait_ge(sem("L1b_exp"), Cg.made())
                        nc.tensor.transpose(bank_c[:, 0, 0:P], p1["L1b"][:], ident[:]).then_inc(sem("L1b_turned"), 1)

                def product_L1a():
                    if B.live:
                        pe.wait_ge(sem("L1a_pT"), B.made())
                        for c in range(C1):
                            bank, at = c // (C1 // 2), c % (C1 // 2)
                            last = mm(bank_b[:, bank, at * P:(at + 1) * P], xl[:, c * P:(c + 1) * P],
                                      pTB[:, c * P // F1, :], start=(at == 0), stop=(at == C1 // 2 - 1))
                            if at == C1 // 2 - 1:
                                last.then_inc(sem(f"L1a_out{bank}"), 1)

                def product_L1b():
                    if Cg.live:
                        product_one("L1b", Cg, bank_c[:, 1, :])

                turn_h1()
                scores_L0()
                project_L1b_first()
                project_L1a()
                turn_exp_L0()
                turn_exp_L3()
                product_L0()
                product_L3()
                scores_L1a()
                scores_L2()
                turn_h3()
                project_L1b_last()
                project_L3()
                scores_L1b()
                turn_exp_L2()
                turn_prob_L1a()
                scores3(0)
                product_L2()
                turn_exp_L1b()
                product_L1a()
                product_L1b()
                scores3(1)

            run_turns(pe, G, turn)

        @block.scalar
        def _(act):
            activation = nc.scalar.activation

            act.wait_ge(sem("setup_one"), 1)
            activation(ones_r[:], one_col[:], ACT.Copy).then_inc(sem("setup_pe"), 1)

            def norm(layer, g, free):
                src = {0: x_in[:, g.slot(XR), :], 1: x1[:, g.slot(X1R), :], 2: x2[:], 3: x3[:, g.slot(X3R), :]}[layer]
                act.wait_ge(sem(f"rs_made{layer}"), g.made())
                act.wait_ge(sem(free[0]), g.made(free[1]))
                activation(h[layer][:, 0, :], src, ACT.Relu, bias=rs[layer][:, 2:3], scale=rs[layer][:, 1:2])\
                    .then_inc(sem(f"h_made{layer}"), 1)

            def exp_one(key, g):
                act.wait_ge(sem(f"{key}_min"), g.made())
                act.wait_ge(sem(f"{key}_turned"), g.made(1))
                act.wait_ge(sem(f"{key}_recip"), g.made(1))
                activation(p1[key][:], nl1[key][:], ACT.Exp, bias=nm1[key][:], scale=-1.0,
                           accum_out=sum1[key][:, 0:1]).then_inc(sem(f"{key}_exp"), 1)

            def pT_one(key, g, bank):
                act.wait_ge(sem(f"{key}_turned"), g.made())
                act.wait_ge(sem(f"{key}_out"), g.made(1))
                activation(pT_hi[key][:], bank, ACT.Copy).then_inc(sem(f"{key}_pT_hi"), 1)

            def v_high(key, g, values, made):
                act.wait_ge(sem(made), g.made())
                act.wait_ge(sem(f"{key}_out"), g.made(1))
                activation(v_hi[key][:], values, ACT.Copy).then_inc(sem(f"{key}_v_hi"), 1)

            def turn(t):
                N0, A, B, Cg, Dg, E, Z = [t.graph(k) for k in range(7)]

                def split_weights(*steps):
                    for n in prepared[t.step] if t.loop is None and t.step in steps else ():
                        (hi, _, src), (e_hi, _, e_src) = w_parts(*w_chunks[n], n)
                        act.wait_ge(sem(f"w_in{n % WR}"), 16 * (n // WR + 1))
                        activation(hi, src, ACT.Copy).then_inc(sem("w_hi"), 1)
                        act.wait_ge(sem("ext_made"), n + 1)
                        activation(e_hi, e_src, ACT.Copy).then_inc(sem("w_hi"), 1)

                def pT_L3():
                    if Z.live:
                        for i in range(2):
                            act.wait_ge(sem(f"L3_turned{i}"), Z.made())
                            act.wait_ge(sem("L3_out"), Z.made(1))
                            activation(pTE[:, i * HB:(i + 1) * HB, :],
                                       bank_e[:, i, :].rearrange("p (k n) -> p k n", k=HB), ACT.Copy)\
                                .then_inc(sem(f"L3_pT{i}"), 1)

                def norm2():
                    if Dg.live:
                        norm(2, Dg, ("L2_out", 1))

                def exp_L0():
                    if A.live:
                        exp_one("L0", A)

                def hT_hi_L1a():
                    if B.live:
                        act.wait_ge(sem("L1a_hT"), B.made())
                        act.wait_ge(sem("L1a_xl"), B.made(1))
                        activation(hT_hi[1][:], bank_b[:, 2, :], ACT.Copy).then_inc(sem("L1a_hT_hi"), 1)

                def pT_L0():
                    if A.live:
                        pT_one("L0", A, bank_a[:, 0:P])

                def hT_hi_L3():
                    if E.live:
                        act.wait_ge(sem("L3_hT"), E.made())
                        act.wait_ge(sem("L3_xl"), E.made(1))
                        activation(hT_hi[3][:], bank_e[:, 0, :], ACT.Copy).then_inc(sem("L3_hT_hi"), 1)

                def relu_L3():
                    if Z.live:
                        act.wait_ge(sem("out_read"), Z.made())
                        activation(rE[:], rE[:], ACT.Relu).then_inc(sem("rE_relu"), 1)

                def norm0():
                    if N0.live:
                        norm(0, N0, ("L0_v_lo", 1))

                def norm1():
                    if A.live:
                        norm(1, A, ("L1a_hT", 1))

                def v_hi_L0():
                    if A.live:
                        v_high("L0", A, h[0][:, 0, :], "h_made0")

                def v_hi_L1b():
                    if Cg.live:
                        v_high("L1b", Cg, xl2[:, 0:D], "xl2_made")

                def v_hi_L2():
                    if Dg.live:
                        v_high("L2", Dg, h[2][:, 0, :], "h_made2")

                def exp_L2():
                    if Dg.live:
                        exp_one("L2", Dg)

                def pT_L2():
                    if Dg.live:
                        pT_one("L2", Dg, bank_a[:, 0:P])

                def exp_L1a():
                    if B.live:
                        act.wait_ge(sem("L1a_min"), B.made())
                        act.wait_ge(sem("L1a_turned"), B.made(1))
                        act.wait_ge(sem("L1a_recip"), B.made(1))
                        for k in range(H1):
                            last = activation(dB[:, k, :], nlB[:, k, :], ACT.Exp, bias=nmB[:, k:k + 1], scale=-1.0,
                                              accum_out=sumB[:, 0, k:k + 1])
                        last.then_inc(sem("L1a_exp"), 1)

                def t_hi_L3():
                    if E.live:
                        act.wait_ge(sem("st3_made"), E.made())
                        act.wait_ge(sem("L3_diag"), E.made(1))
                        activation(t3_hi[:], st3[:, 1, HB:H3], ACT.Copy).then_inc(sem("t3_hi_made"), 1)

                def values_L3():
                    if E.live:
                        act.wait_ge(sem("st3_made"), E.made())
                        act.wait_ge(sem("L3_out"), E.made(1))
                        src = bank_e[:, :, 0:D // 2].rearrange("p b (k n) -> p b k n", k=HB)
                        activation(xa_heads[:, :, 0:K3].rearrange("p (b k) n -> p b k n", b=2), src, ACT.Copy)\
                            .then_inc(sem("xa_made"), 1)

                def exp_L1b():
                    if Cg.live:
                        exp_one("L1b", Cg)

                def pT_L1a():
                    if B.live:
                        act.wait_ge(sem("L1a_turned"), B.made())
                        act.wait_ge(sem("L1a_out1"), B.made(1))
                        activation(pTB[:], bank_b[:, 2, :].rearrange("p (k n) -> p k n", k=H1), ACT.Copy)\
                            .then_inc(sem("L1a_pT"), 1)

                def pT_L1b():
                    if Cg.live:
                        pT_one("L1b", Cg, bank_c[:, 0, 0:P])

                def norm3():
                    if E.live:
                        norm(3, E, ("L3_hT", 1))

                def elu_exp(i):
                    if B.live:
                        act.wait_ge(sem(f"L1a_out{i}"), B.made())
                        act.wait_ge(sem(("g_made_first", "g_made_last")[i]), B.made(1))
                        half = slice(i * (C1 // 2), (i + 1) * (C1 // 2))
                        activation(elu[:, half, :], bank_b[:, i, :].rearrange("p (c n) -> p c n", c=C1 // 2),
                                   ACT.Exp).then_inc(sem(f"elu_exp{i}"), 1)
                        act.wait_ge(sem(f"elu_exp{i}"), B.made())
                        activation(elu[:, half, :], elu[:, half, :], ACT.Relu, bias=1.0, scale=-1.0)\
                            .then_inc(sem(f"elu_below{i}"), 1)

                def g_high(i):
                    if B.live:
                        act.wait_ge(sem(("g_made_first", "g_made_last")[i]), B.made())
                        act.wait_ge(sem("L1b_xl"), B.made(1))
                        half = slice(i * (C1 // 2), (i + 1) * (C1 // 2))
                        activation(g_hi[:, half, :], g1[:, half, :], ACT.Copy).then_inc(sem(f"g_hi{i}"), 1)

                def exp3(i):
                    g = (E, Z)[i]
                    if g.live:
                        act.wait_ge(sem(f"L3_shifted{i}"), g.made())
                        act.wait_ge(sem(f"L3_turned{i}"), g.made(1))
                        activation(pE[:, i * HB:(i + 1) * HB, :], nlE[:, i * HB:(i + 1) * HB, :], ACT.Exp,
                                   scale=-1.0).then_inc(sem(f"L3_exp{i}"), 1)

                hT_hi_L1a()
                split_weights(0, 1)
                exp_L0()
                v_hi_L0()
                norm2()
                norm3()
                exp3(1)
                pT_L0()
                pT_L3()
                v_hi_L2()
                split_weights(2, 3)
                hT_hi_L3()
                relu_L3()
                norm1()
                exp_L1a()
                exp_L2()
                norm0()
                t_hi_L3()
                values_L3()
                pT_L2()
                pT_L1a()
                exp_L1b()
                v_hi_L1b()
                pT_L1b()
                elu_exp(0)
                elu_exp(1)
                g_high(0)
                g_high(1)
                exp3(0)

            run_turns(act, G, turn)

        @block.vector
        def _(dve):
            tt, ts, stt = nc.vector.tensor_tensor, nc.vector.tensor_scalar, nc.vector.scalar_tensor_tensor

            nc.vector.memset(ext[:], 0.0).then_inc(sem("ext_zero"), 1)
            nc.vector.memset(nhalf[:], -0.5).then_inc(sem("setup_pool"), 1)
            nc.vector.memset(one_col[:], 1.0).then_inc(sem("setup_one"), 1)
            nc.vector.memset(xa[:], 1.0).then_inc(sem("setup_pe"), 1)
            nc.vector.memset(b1_row[:, D1:E1], 0.0).then_inc(sem("rows_made"), 1)
            nc.vector.memset(b2_row[:, D:E2], 0.0).then_inc(sem("rows_made"), 1)
            dve.wait_ge(sem("ext_zero"), 1)

            def stats(layer, g, src):
                nc.vector.bn_stats(bn[layer][:], src).then_inc(sem(f"bn_made{layer}"), 1)
                dve.wait_ge(sem(f"bn_made{layer}"), g.made())
                dve.wait_ge(sem(f"rs_made{layer}"), g.made(1))
                dve.sem_inc(sem("passed_dve"), 1)
                nc.vector.bn_aggr(mv[layer][:], bn[layer][:]).then_inc(sem(f"mv_made{layer}"), 1)

            def score_columns(layer, g, scores):
                dve.wait_ge(sem(f"h_made{layer}"), g.made())
                dve.wait_ge(sem(scores), g.made(1))
                for i, row in enumerate((s_row, t_row)):
                    last = nc.vector.tensor_tensor_reduce(product[:, layer + i, :], h[layer][:, 0, :], row[layer][:], 1.0, 0.0,
                                                          ALU.mult, ALU.add, st[layer][:, i:i + 1])
                last.then_inc(sem(f"st_made{layer}"), 1)

            def softmax_one(key, g, bank, ns, bias=None):
                dve.wait_ge(sem(f"{key}_scores"), g.made())
                dve.wait_ge(sem(f"{key}_exp"), g.made(1))
                if bias is None:
                    ts(nl1[key][:], bank, ns, None, ALU.add).then_inc(sem(f"{key}_v"), 1)
                else:
                    ts(nl1[key][:], bank, ns, bias, ALU.add, ALU.subtract).then_inc(sem(f"{key}_v"), 1)
                dve.wait_ge(sem(f"{key}_v"), g.made())
                stt(nl1[key][:], nl1[key][:], SLOPE, nl1[key][:], ALU.mult, ALU.min)\
                    .then_inc(sem(f"{key}_nl"), 1)
                dve.wait_ge(sem(f"{key}_nl"), g.made())
                nc.vector.tensor_reduce(nm1[key][:], nl1[key][:], AX_X, ALU.min).then_inc(sem(f"{key}_min"), 1)

            def recip_one(key, g):
                dve.wait_ge(sem(f"{key}_exp"), g.made())
                nc.vector.reciprocal(sum1[key][:, 1:2], sum1[key][:, 0:1]).then_inc(sem(f"{key}_recip"), 1)

            def pT_low(key, g, bank):
                dve.wait_ge(sem(f"{key}_pT_hi"), g.made())
                dve.wait_ge(sem(f"{key}_out"), g.made(1))
                tt(pT_lo[key][:], bank, pT_hi[key][:].bitcast(F32), ALU.subtract).then_inc(sem(f"{key}_pT_lo"), 1)

            def residual(key, g, bank, src, dst, made):
                dve.wait_ge(sem(f"{key}_out"), g.made())
                dve.wait_ge(sem(f"{key}_recip"), g.made())
                stt(dst, bank, sum1[key][:, 1:2], src, ALU.mult, ALU.add).then_inc(sem(made), 1)

            def turn(t):
                N0, A, B, Cg, Dg, E, Z = [t.graph(k) for k in range(7)]

                def split_weights(*steps):
                    for n in prepared[t.step] if t.loop is None and t.step in steps else ():
                        kind, c = w_chunks[n]
                        heads, att, at = w_att_of[kind]
                        k = w_cols[kind] // heads
                        if c == 0:
                            dve.wait_ge(sem({"w1": "att1_in", "w2": "att2_in", "w3": "att3_in"}[kind]), 32)
                        dve.wait_ge(sem(f"w_in{n % WR}"), 16 * (n // WR + 1))
                        if n:
                            dve.wait_ge(sem("ext_made"), n)
                        if t.step:
                            dve.wait_ge(sem("st_made0"), t.step)
                        for i, sign in enumerate((-1.0, 1.0)):
                            for head in range(heads):
                                col, cols = at + i * heads + head, slice(head * k, (head + 1) * k)
                                last = nc.vector.tensor_tensor_reduce(
                                    scratch[:, i * heads * k + head * k:i * heads * k + (head + 1) * k],
                                    staged[n][:, cols], att[i][:, cols], sign, 0.0,
                                    ALU.mult, ALU.add, ext[:, n % WR, col:col + 1])
                        last.then_inc(sem("ext_made"), 1)
                        if n == prepared[t.step][-1]:
                            dve.wait_ge(sem("ext_made"), n + 1)

                def make_rows():
                    if t.loop is None and t.step == 0:
                        dve.wait_ge(sem("ident_loaded"), 16)
                        ts(nident[:], ident[:], -1.0, None, ALU.mult).then_inc(sem("setup_pe"), 1)
                        nc.vector.tensor_copy(identb[:], ident[:]).then_inc(sem("setup_pe"), 1)
                        ts(offdiag[:], ident[:], -1.0, 1.0, ALU.mult, ALU.add).then_inc(sem("setup_pool"), 1)
                        dve.wait_ge(sem("u0_made"), 1)
                        ts(s_row[0][:], bank_e[:, 0, :], -1.0, None, ALU.mult).then_inc(sem("rows_made"), 1)
                        nc.vector.tensor_copy(t_row[0][:], bank_e[:, 1, :]).then_inc(sem("rows_made"), 1)
                        dve.wait_ge(sem("rows_made"), 4)
                    if t.loop is None and t.step == 1:
                        dve.wait_ge(sem("rows_in"), 16 * 6)
                        ts(s_row[2][:], s_row[2][:], -1.0, None, ALU.mult).then_inc(sem("rows_made"), 1)
                        dve.wait_ge(sem("rows_made"), 5)

                def stats_2():
                    if Cg.live:
                        dve.wait_ge(sem("x2_made"), Cg.made())
                        stats(2, Cg, x2[:])

                def min_L0():
                    if A.live:
                        softmax_one("L0", A, bank_a[:, 0:P], st[0][:, 0:1])

                def result_L3():
                    if Z.live:
                        dve.wait_ge(sem("L3_out"), Z.made())
                        wide = bank_e[:, :, 0:HB * KA].rearrange("p b (k n) -> p b k n", k=HB)
                        nc.vector.reciprocal(rcE[:], wide[:, :, :, K3]).then_inc(sem("L3_recip"), 1)
                        dve.wait_ge(sem("L3_recip"), Z.made())
                        dve.wait_ge(sem("out_made"), Z.made(1))
                        r4 = rE[:].rearrange("p (b k n) -> p b k n", b=2, k=HB)
                        rc4 = rcE[:].rearrange("p b (k a) -> p b k a", a=1).to_broadcast([P, 2, HB, K3])
                        tt(r4, wide[:, :, :, 0:K3], rc4, ALU.mult).then_inc(sem("out_read"), 1)

                def pT_lo_L0():
                    if A.live:
                        pT_low("L0", A, bank_a[:, 0:P])

                def pT_lo_L1b():
                    if Cg.live:
                        pT_low("L1b", Cg, bank_c[:, 0, 0:P])

                def pT_lo_L2():
                    if Dg.live:
                        pT_low("L2", Dg, bank_a[:, 0:P])

                def columns_L2():
                    if Dg.live:
                        score_columns(2, Dg, "L2_scores")

                def hT_lo_L1a():
                    if B.live:
                        dve.wait_ge(sem("L1a_hT_hi"), B.made())
                        dve.wait_ge(sem("L1a_xl"), B.made(1))
                        tt(hT_lo[1][:], bank_b[:, 2, :], hT_hi[1][:].bitcast(F32), ALU.subtract)\
                            .then_inc(sem("L1a_hT_lo"), 1)

                def recip_L0():
                    if A.live:
                        recip_one("L0", A)

                def stats_0():
                    if N0.live:
                        dve.wait_ge(sem(f"x_loaded{N0.slot(XR)}"), N0.turns_of(XR, 32))
                        stats(0, N0, x_in[:, N0.slot(XR), :])

                def columns_L0():
                    if N0.live:
                        score_columns(0, N0, "L0_scores")

                def values_L1a():
                    if B.live:
                        if t.loop is None and t.step == 2:
                            dve.wait_ge(sem("w_split"), C + C1)
                        dve.wait_ge(sem("L1a_xl"), B.made())
                        dve.wait_ge(sem("L1a_out1"), B.made(1))
                        tt(xl[:].rearrange("p (b n) -> p b n", b=3), bank_b[:, :, 0:B1],
                           b1_row[:].rearrange("p (b n) -> p b n", b=3), ALU.add).then_inc(sem("xl_made"), 1)

                def residual_L0():
                    if A.live:
                        dve.wait_ge(sem("h_made1"), A.made(3))
                        residual("L0", A, bank_a[:], x_in[:, A.slot(XR), :], x1[:, A.slot(X1R), :], "x1_made")

                def stats_1():
                    if A.live:
                        dve.wait_ge(sem("x1_made"), A.made())
                        stats(1, A, x1[:, A.slot(X1R), :])

                def hT_lo_L3():
                    if E.live:
                        dve.wait_ge(sem("L3_hT_hi"), E.made())
                        dve.wait_ge(sem("L3_xl"), E.made(1))
                        tt(hT_lo[3][:], bank_e[:, 0, :], hT_hi[3][:].bitcast(F32), ALU.subtract)\
                            .then_inc(sem("L3_hT_lo"), 1)

                def min_L1a():
                    if B.live:
                        dve.wait_ge(sem("L1a_scores"), B.made())
                        dve.wait_ge(sem("L1a_exp"), B.made(1))
                        ns = xl[:, D1:D1 + H1].rearrange("p (h a) -> p h a", a=1).to_broadcast([P, H1, P])
                        tt(nlB[:], bank_b[:, 2, :].rearrange("p (h n) -> p h n", h=H1), ns, ALU.add)\
                            .then_inc(sem("L1a_v"), 1)
                        dve.wait_ge(sem("L1a_v"), B.made())
                        stt(nlB[:], nlB[:], SLOPE, nlB[:], ALU.mult, ALU.min).then_inc(sem("L1a_nl"), 1)
                        dve.wait_ge(sem("L1a_nl"), B.made())
                        nc.vector.tensor_reduce(nmB[:], nlB[:], AX_X, ALU.min).then_inc(sem("L1a_min"), 1)

                def min_L2():
                    if Dg.live:
                        softmax_one("L2", Dg, bank_a[:, 0:P], st[2][:, 0:1], attn_b_all[:])

                def recip_L1a():
                    if B.live:
                        dve.wait_ge(sem("L1a_exp"), B.made())
                        dve.wait_ge(sem("L1a_prob"), B.made(1))
                        nc.vector.reciprocal(sumB[:, 1, :], sumB[:, 0, :]).then_inc(sem("L1a_recip"), 1)

                def recip_L2():
                    if Dg.live:
                        recip_one("L2", Dg)

                def values_L1b():
                    if Cg.live:
                        dve.wait_ge(sem("L1b_xl"), Cg.made())
                        dve.wait_ge(sem("L1b_out"), Cg.made(1))
                        tt(xl2[:].rearrange("p (b n) -> p b n", b=2), bank_c[:, :, 0:B2],
                           b2_row[:].rearrange("p (b n) -> p b n", b=2), ALU.add).then_inc(sem("xl2_made"), 1)

                def columns_L3():
                    if E.live:
                        dve.wait_ge(sem("L3_xl"), E.made())
                        dve.wait_ge(sem("L3_scores0"), E.made(1))
                        dve.wait_ge(sem("L3_v1"), E.made(1))
                        dve.wait_ge(sem("L3_diag"), E.made(1))
                        tt(st3[:, 0, :], bank_e[:, 0, D // 2:B3], b_att_all[:], ALU.subtract).then_inc(sem("st3_s"), 1)
                        nc.vector.tensor_copy(st3[:, 1, :], bank_e[:, 1, D // 2:B3]).then_inc(sem("st3_made"), 1)

                def residual_L2():
                    if Dg.live:
                        dve.wait_ge(sem("out_made"), Dg.made(2))
                        residual("L2", Dg, bank_a[:], x2[:], x3[:, Dg.slot(X3R), :], "x3_made")

                def stats_3():
                    if E.live:
                        dve.wait_ge(sem("x3_made"), E.made())
                        stats(3, E, x3[:, E.slot(X3R), :])

                def min_L1b():
                    if Cg.live:
                        softmax_one("L1b", Cg, bank_c[:, 0, 0:P], xl2[:, D:D + 1])

                def v_L3(i):
                    if E.live:
                        dve.wait_ge(sem(f"L3_scores{i}"), E.made())
                        dve.wait_ge(sem(f"L3_exp{i}"), E.made(1))
                        dve.wait_ge(sem("st3_s"), E.made())
                        half = slice(i * HB, (i + 1) * HB)
                        ns = st3[:, 0, half].rearrange("p (h a) -> p h a", a=1).to_broadcast([P, HB, P])
                        tt(nlE[:, half, :], bank_e[:, i, :].rearrange("p (h n) -> p h n", h=HB), ns, ALU.add)\
                            .then_inc(sem(f"L3_v{i}"), 1)

                def recip_L1b():
                    if Cg.live:
                        recip_one("L1b", Cg)

                def nl_L3(i):
                    g = (E, Z)[i]
                    if g.live:
                        dve.wait_ge(sem(f"L3_v{i}"), g.made())
                        half = slice(i * HB, (i + 1) * HB)
                        stt(nlE[:, half, :], nlE[:, half, :], SLOPE, nlE[:, half, :], ALU.mult, ALU.min)\
                            .then_inc(sem(f"L3_nl{i}"), 1)

                def min_L3(i):
                    g = (E, Z)[i]
                    if g.live:
                        dve.wait_ge(sem(f"L3_nl{i}"), g.made())
                        half = slice(i * HB, (i + 1) * HB)
                        nc.vector.tensor_reduce(nmE[:, half], nlE[:, half, :], AX_X, ALU.min)\
                            .then_inc(sem(f"L3_min{i}"), 1)

                def elu_L1a(i, name):
                    if B.live:
                        half = slice(i * (C1 // 2), (i + 1) * (C1 // 2))
                        dve.wait_ge(sem(f"elu_below{i}"), B.made())
                        dve.wait_ge(sem("g_lo_last"), B.made(1))
                        stt(g1[:, half, :], bank_b[:, i, :].rearrange("p (c n) -> p c n", c=C1 // 2), 0.0,
                            elu[:, half, :], ALU.max, ALU.subtract).then_inc(sem(name), 1)

                def g_lo_first():
                    if B.live:
                        dve.wait_ge(sem("g_hi0"), B.made())
                        half = slice(0, C1 // 2)
                        tt(g_lo[:, half, :], g1[:, half, :], g_hi[:, half, :].bitcast(F32), ALU.subtract)\
                            .then_inc(sem("g_lo_first"), 1)

                def residual_L1b():
                    if Cg.live:
                        dve.wait_ge(sem("h_made2"), Cg.made(1))
                        dve.wait_ge(sem("x3_made"), Cg.made(1))
                        residual("L1b", Cg, bank_c[:, 1, :], x1[:, Cg.slot(X1R), :], x2[:], "x2_made")

                split_weights(0, 1)
                make_rows()
                hT_lo_L1a()
                min_L0()
                stats_3()
                nl_L3(1)
                min_L3(1)
                columns_L2()
                stats_0()
                recip_L0()
                split_weights(2, 3)
                pT_lo_L0()
                values_L1a()
                residual_L0()
                result_L3()
                stats_1()
                min_L1a()
                hT_lo_L3()
                min_L2()
                recip_L1a()
                values_L1b()
                columns_L3()
                recip_L2()
                min_L1b()
                pT_lo_L2()
                columns_L0()
                v_L3(0)
                pT_lo_L1b()
                recip_L1b()
                residual_L2()
                nl_L3(0)
                min_L3(0)
                elu_L1a(0, "g_made_first")
                residual_L1b()
                elu_L1a(1, "g_made_last")
                g_lo_first()
                stats_2()
                v_L3(1)

            run_turns(dve, G, turn)

        @block.gpsimd
        def _(pool):
            tt, ts = nc.gpsimd.tensor_tensor, nc.gpsimd.tensor_scalar

            def scale_and_bias(layer, g):
                pool.wait_ge(sem(f"mv_made{layer}"), g.made())
                pool.wait_ge(sem(f"h_made{layer}"), g.made(1))
                pool.sem_inc(sem("passed_pool"), 1)
                v, r, b = [rs[layer][:, k:k + 1] for k in range(3)]
                ts(v, mv[layer][:, 1:2], EPS, None, ALU.add).then_inc(sem(f"var_made{layer}"), 1)
                pool.wait_ge(sem(f"var_made{layer}"), g.made())
                tt(r, v, nhalf[:], ALU.pow).then_inc(sem(f"rstd_made{layer}"), 1)
                pool.wait_ge(sem(f"rstd_made{layer}"), g.made())
                pool.sem_inc(sem("passed_pool"), 1)
                ts(b, mv[layer][:, 0:1], r, -1.0, ALU.mult, ALU.mult).then_inc(sem(f"rs_made{layer}"), 1)

            def turn(t):
                N0, A, B, Cg, Dg, E, Z = [t.graph(k) for k in range(7)]

                def split_weights(*steps):
                    for n in prepared[t.step] if t.loop is None and t.step in steps else ():
                        pool.wait_ge(sem(f"w_in{n % WR}"), 16 * (n // WR + 1))
                        pool.wait_ge(sem("ext_made"), n + 1)
                        pool.wait_ge(sem("w_hi"), 2 * n + 2)
                        for hi, lo, src in w_parts(*w_chunks[n], n):
                            last = tt(lo, src, hi.bitcast(F32), ALU.subtract)
                        last.then_inc(sem("w_split"), 1)

                def norm_2():
                    if Dg.live:
                        scale_and_bias(2, Dg)

                def norm_0_masks():
                    if N0.live:
                        if t.loop is None and t.step == 0:
                            pool.wait_ge(sem("setup_pool"), 2)
                        scale_and_bias(0, N0)
                        s, m = N0.slot(XR), N0.slot(MR)
                        pool.wait_ge(sem(f"x_loaded{s}"), N0.turns_of(XR, 32))
                        pool.wait_ge(sem("L3_scores1"), N0.made(MR))
                        pool.sem_inc(sem("passed_pool"), 1)
                        ts(mask[:, m, :], adj_in[:, s, :], -BIG, BIG, ALU.mult, ALU.add).then_inc(sem("mask_made"), 1)
                        pool.wait_ge(sem("mask_made"), N0.made())
                        tt(mask_loop[:, m, :], mask[:, m, :], offdiag[:], ALU.mult).then_inc(sem("masks_made"), 1)

                def diag_L3():
                    if E.live:
                        pool.wait_ge(sem("t3_hi_made"), E.made())
                        pool.wait_ge(sem("L3_diag"), E.made(1))
                        tt(t3_lo[:], st3[:, 1, HB:H3], t3_hi[:].bitcast(F32), ALU.subtract).then_inc(sem("t3_lo_made"), 1)
                        pool.wait_ge(sem("t3_lo_made"), E.made())
                        if B.live:
                            pool.wait_ge(sem("L1a_xl"), B.made())
                        nid = nident[:].rearrange("p (a n) -> p a n", a=1).to_broadcast([P, HB, P])
                        for diag, part in ((diag_hi, t3_hi[:].bitcast(F32)), (diag_lo, t3_lo[:])):
                            t_all = part.rearrange("p (h a) -> p h a", a=1).to_broadcast([P, HB, P])
                            last = tt(diag, nid, t_all, ALU.mult)
                        last.then_inc(sem("L3_diag"), 1)

                def out_L3():
                    if Z.live:
                        pool.wait_ge(sem("rE_relu"), Z.made())
                        pool.wait_ge(sem(f"out_stored{Z.slot(OR)}"), Z.turns_of(OR, 16, OR))
                        tt(out_sb[:, Z.slot(OR), :], rE[:], x3[:, Z.slot(X3R), :], ALU.add).then_inc(sem("out_made"), 1)

                def norm_1():
                    if A.live:
                        scale_and_bias(1, A)

                def prob_L1a():
                    if B.live:
                        pool.wait_ge(sem("L1a_recip"), B.made())
                        rc = sumB[:, 1, :].rearrange("p (h a) -> p h a", a=1).to_broadcast([P, H1, P])
                        tt(dB[:], dB[:], rc, ALU.mult).then_inc(sem("L1a_prob"), 1)

                def v_low(key, g, values):
                    pool.wait_ge(sem(f"{key}_v_hi"), g.made())
                    pool.wait_ge(sem(f"{key}_out"), g.made(1))
                    tt(v_lo[key][:], values, v_hi[key][:].bitcast(F32), ALU.subtract)\
                        .then_inc(sem(f"{key}_v_lo"), 1)

                def v_lo_L0():
                    if A.live:
                        v_low("L0", A, h[0][:, 0, :])

                def v_lo_L1b():
                    if Cg.live:
                        v_low("L1b", Cg, xl2[:, 0:D])

                def v_lo_L2():
                    if Dg.live:
                        v_low("L2", Dg, h[2][:, 0, :])

                def norm_3():
                    if E.live:
                        scale_and_bias(3, E)

                def shift_L3(i):
                    g = (E, Z)[i]
                    if g.live:
                        half = slice(i * HB, (i + 1) * HB)
                        pool.wait_ge(sem(f"L3_min{i}"), g.made())
                        nm = nmE[:, half].rearrange("p (h a) -> p h a", a=1).to_broadcast([P, HB, P])
                        tt(nlE[:, half, :], nlE[:, half, :], nm, ALU.subtract).then_inc(sem(f"L3_shifted{i}"), 1)

                def g_lo_last():
                    if B.live:
                        pool.wait_ge(sem("g_hi1"), B.made())
                        pool.wait_ge(sem("L1b_xl"), B.made(1))
                        half = slice(C1 // 2, C1)
                        tt(g_lo[:, half, :], g1[:, half, :], g_hi[:, half, :].bitcast(F32), ALU.subtract)\
                            .then_inc(sem("g_lo_last"), 1)

                split_weights(0, 1)
                norm_2()
                norm_3()
                shift_L3(1)
                v_lo_L0()
                norm_0_masks()
                split_weights(2, 3)
                norm_1()
                v_lo_L2()
                out_L3()
                prob_L1a()
                diag_L3()
                v_lo_L1b()
                shift_L3(0)
                g_lo_last()

            run_turns(pool, G, turn)


_INS = ["x", "adj", "L0_gnn_W", "L0_gnn_a1", "L0_gnn_a2", "L1_gnn_W1", "L1_gnn_att_src1", "L1_gnn_att_dst1",
        "L1_gnn_b1", "L1_gnn_W2", "L1_gnn_att_src2", "L1_gnn_att_dst2", "L1_gnn_b2", "L2_gnn_attn_w_src",
        "L2_gnn_attn_w_dst", "L2_gnn_attn_b", "L3_gnn_W_proj", "L3_gnn_W_att", "L3_gnn_b_att"]


def kernel(**inputs):
    import concourse.bacc as bacc
    import numpy as np
    from concourse.bass_utils import run_bass_kernel_spmd

    nc = bacc.Bacc("TRN2", target_bir_lowering=False, num_devices=1)
    ins = {f"in_{name}": np.ascontiguousarray(inputs[name]) for name in _INS}
    ins["in_ident"] = np.eye(P, dtype=np.float32)
    aps = [nc.dram_tensor(n, a.shape, mybir.dt.from_np(a.dtype), kind="ExternalInput").ap() for n, a in ins.items()]
    out = nc.dram_tensor("out", inputs["x"].shape, F32, kind="ExternalOutput").ap()
    build(nc, *aps, out)
    r = run_bass_kernel_spmd(nc, [ins], core_ids=[0])
    return r.results[0]["out"]
```
